# Optimizing a Trainium2 kernel written in Bass

```python
import numpy as np
import jax
import jax.numpy as jnp

def _softmax(x, axis=-1):
    return jax.nn.softmax(x, axis=axis)

def _gelu(x):
    return jax.nn.gelu(x, approximate=True)

def _silu(x):
    return jax.nn.silu(x)

def _sigmoid(x):
    return jax.nn.sigmoid(x)

def _layernorm(x, axis=-1, eps=1e-05):
    m = jnp.mean(x, axis=axis, keepdims=True)
    v = jnp.var(x, axis=axis, keepdims=True)
    return (x - m) / jnp.sqrt(v + eps)

def _scatter_add(tgt, idx, src, axis=0):
    return tgt.at[idx].add(src)

def _segment_sum(src, seg, n):
    return jax.ops.segment_sum(src, seg, n)
kernel_name = 'mk_sandwich_d1_jaxref_r8_64f40e'

def setup_inputs(seed: int=0):
    np.random.seed(seed)
    _w = jnp.asarray

    def _L0_attn_setup():
        import jax, jax.numpy as jnp
        import numpy as np
        B, S, DIM, H = (2, 256, 128, 16)
        D = DIM // H

        def _xavier(key, shape):
            a = float(np.sqrt(6.0 / (shape[0] + shape[1])))
            return jax.random.uniform(key, shape, minval=-a, maxval=a, dtype=jnp.float32)

        def _split_heads(t):
            b, s, _ = t.shape
            return t.reshape(b, s, H, D).transpose(0, 2, 1, 3).reshape(b * H, s, D)
        key = jax.random.key(seed)
        ks = jax.random.split(key, 8)
        x = jax.random.normal(ks[0], (B, S, DIM), dtype=jnp.float32)
        Wq = _xavier(ks[1], (DIM, DIM))
        Wk = _xavier(ks[2], (DIM, DIM))
        Wv = _xavier(ks[3], (DIM, DIM))
        Wo = _xavier(ks[4], (DIM, DIM))
        bq = jax.random.normal(ks[5], (DIM,), dtype=jnp.float32) * 0.02
        bk = jax.random.normal(ks[6], (DIM,), dtype=jnp.float32) * 0.02
        bv = jax.random.normal(ks[7], (DIM,), dtype=jnp.float32) * 0.02
        bo = jnp.zeros((DIM,), dtype=jnp.float32)
        return {'x': x, 'Wq': Wq, 'bq': bq, 'Wk': Wk, 'bk': bk, 'Wv': Wv, 'bv': bv, 'Wo': Wo, 'bo': bo}
    _L0_attn_in = _L0_attn_setup()

    def _L0_ffn_setup():
        import jax, jax.numpy as jnp
        import numpy as np
        EPS = 1e-12

        def rms_norm(t, gamma):
            n = jnp.maximum(jnp.linalg.norm(t, axis=-1, keepdims=True), EPS)
            scale = jnp.sqrt(jnp.asarray(t.shape[-1], t.dtype))
            return t / n * scale * gamma
        key = jax.random.key(seed)
        ks = jax.random.split(key, 4)
        b, s, d = (4, 512, 128)
        e, t = (8, 64)
        hidden = 4 * d
        return {'x': jax.random.normal(ks[0], (b, s, d), dtype=jnp.float32), 'gamma_x': jnp.ones((d,), dtype=jnp.float32), 'gamma_slot': jnp.ones((d,), dtype=jnp.float32), 'slot_embeds': jax.random.normal(ks[1], (e, t, d), dtype=jnp.float32), 'w1': jax.random.normal(ks[2], (d, hidden), dtype=jnp.float32) * (1.0 / np.sqrt(d)), 'w2': jax.random.normal(ks[3], (hidden, d), dtype=jnp.float32) * (1.0 / np.sqrt(hidden))}
    _L0_ffn_in = _L0_ffn_setup()
    _d = {'L0_attn_x': _L0_attn_in['x'], 'L0_attn_Wq': _L0_attn_in['Wq'], 'L0_attn_bq': _L0_attn_in['bq'], 'L0_attn_Wk': _L0_attn_in['Wk'], 'L0_attn_bk': _L0_attn_in['bk'], 'L0_attn_Wv': _L0_attn_in['Wv'], 'L0_attn_bv': _L0_attn_in['bv'], 'L0_attn_Wo': _L0_attn_in['Wo'], 'L0_attn_bo': _L0_attn_in['bo'], 'L0_ffn_gamma_x': _L0_ffn_in['gamma_x'], 'L0_ffn_gamma_slot': _L0_ffn_in['gamma_slot'], 'L0_ffn_slot_embeds': _L0_ffn_in['slot_embeds'], 'L0_ffn_w1': _L0_ffn_in['w1'], 'L0_ffn_w2': _L0_ffn_in['w2']}
    _x0 = _d['L0_attn_x']
    _d['L0_attn_x'] = jax.random.normal(jax.random.fold_in(jax.random.key(seed), 1), (32, 256, 128), dtype=_x0.dtype)
    del _x0
    return _d

def reference(L0_attn_x, L0_attn_Wq, L0_attn_bq, L0_attn_Wk, L0_attn_bk, L0_attn_Wv, L0_attn_bv, L0_attn_Wo, L0_attn_bo, L0_ffn_gamma_x, L0_ffn_gamma_slot, L0_ffn_slot_embeds, L0_ffn_w1, L0_ffn_w2):

    def _L0_attn_ref(x, Wq, bq, Wk, bk, Wv, bv, Wo, bo):
        import jax, jax.numpy as jnp
        import numpy as np
        B, S, DIM, H = (2, 256, 128, 16)
        D = DIM // H

        def _xavier(key, shape):
            a = float(np.sqrt(6.0 / (shape[0] + shape[1])))
            return jax.random.uniform(key, shape, minval=-a, maxval=a, dtype=jnp.float32)

        def _split_heads(t):
            b, s, _ = t.shape
            return t.reshape(b, s, H, D).transpose(0, 2, 1, 3).reshape(b * H, s, D)
        b, s, _ = x.shape
        q = _split_heads(x @ Wq.T + bq)
        k = _split_heads(x @ Wk.T + bk)
        v = _split_heads(x @ Wv.T + bv)
        q = jnp.exp(q)
        k = jnp.exp(k)
        kv = jnp.cumsum(k[:, :, :, None] * v[:, :, None, :], axis=1)
        k1 = jnp.cumsum(k, axis=1)
        num = jnp.einsum('zsD,zsDd->zsd', q, kv)
        den = jnp.sum(q * k1, axis=-1, keepdims=True)
        out = num / den
        out = out.reshape(b, H, s, D).transpose(0, 2, 1, 3).reshape(b, s, DIM)
        return out @ Wo.T + bo

    def _L0_ffn_ref(x, gamma_x, gamma_slot, slot_embeds, w1, w2):
        import jax, jax.numpy as jnp
        import numpy as np
        EPS = 1e-12

        def rms_norm(t, gamma):
            n = jnp.maximum(jnp.linalg.norm(t, axis=-1, keepdims=True), EPS)
            scale = jnp.sqrt(jnp.asarray(t.shape[-1], t.dtype))
            return t / n * scale * gamma
        b, s, d = x.shape
        e, t, _ = slot_embeds.shape
        xn = rms_norm(x, gamma_x)
        se = rms_norm(slot_embeds, gamma_slot)
        logits = jnp.einsum('bsd,etd->bset', xn, se)
        dispatch = jax.nn.softmax(logits, axis=1)
        slots = jnp.einsum('bsd,bset->betd', xn, dispatch)
        h = jax.nn.gelu(slots @ w1, approximate=False)
        processed = h @ w2
        combine = jax.nn.softmax(logits.reshape(b, s, e * t), axis=-1)
        out = jnp.einsum('bnd,bsn->bsd', processed.reshape(b, e * t, d), combine)
        return out
    x = L0_attn_x
    x = x + _layernorm(_L0_attn_ref(_layernorm(x, axis=-1), L0_attn_Wq, L0_attn_bq, L0_attn_Wk, L0_attn_bk, L0_attn_Wv, L0_attn_bv, L0_attn_Wo, L0_attn_bo), axis=-1)
    x = x + _layernorm(_L0_ffn_ref(_layernorm(x, axis=-1), L0_ffn_gamma_x, L0_ffn_gamma_slot, L0_ffn_slot_embeds, L0_ffn_w1, L0_ffn_w2), axis=-1)
    return x

_drawn_inputs = setup_inputs


def setup_inputs(seed=0):
    import zlib

    import numpy as np

    out = dict(_drawn_inputs(seed))
    spreads = {'L0_attn_bo': (0.0, 0.1), 'L0_ffn_gamma_x': (1.0, 0.2), 'L0_ffn_gamma_slot': (1.0, 0.2)}
    factors = {'L0_attn_bq': 5.208, 'L0_attn_bk': 5.947}
    for name, (base, spread) in spreads.items():
        noise = np.random.default_rng([zlib.crc32(name.encode()), seed]).standard_normal(out[name].shape)
        drawn = base * np.exp(spread * noise) if base else spread * noise
        out[name] = jnp.asarray(drawn.astype(out[name].dtype))
    for name, factor in factors.items():
        out[name] = (out[name] * factor).astype(out[name].dtype)
    return out
```

```python
import concourse.bass as bass
from concourse import mybir
from contextlib import ExitStack


def attention_and_slot_mixture(
    nc: bass.Bass,
    x: bass.AP, wq: bass.AP, bq: bass.AP, wk: bass.AP, bk: bass.AP, wv: bass.AP, bv: bass.AP,
    wo: bass.AP, bo: bass.AP, gamma_x: bass.AP, gamma_slot: bass.AP, slot_embeds: bass.AP,
    w1: bass.AP, w2: bass.AP, out: bass.AP,
):
    F32 = mybir.dt.float32
    F32R = mybir.dt.float32r
    ALU = mybir.AluOpType
    ACT = mybir.ActivationFunctionType
    AX = mybir.AxisListType

    NB, SEQ, DIM = x.shape
    P = 128
    NC = SEQ // P
    NH = 16
    HD = DIM // NH
    NE, NT, _ = slot_embeds.shape
    SLOTS = NE * NT
    SJ = SLOTS // P
    HID = w1.shape[1]
    FJ = HID // P
    KVF = NH * HD * HD
    FEAT = KVF + DIM
    HALF = KVF // 2
    HH = NH // 2
    QKV = 3 * DIM
    XW = DIM + 2
    NM = SJ + NC
    EPS_LN = 1e-5
    EPS_RMS = 1e-12
    ROOT_DIM = float(DIM) ** 0.5

    x_v = x.rearrange("b (c p) d -> b p c d", p=P)
    out_v = out.rearrange("b (c p) d -> b p c d", p=P)

    ctx = ExitStack()
    with ctx:
        def sb(name, shape, dt=F32):
            return ctx.enter_context(nc.sbuf_tensor(name, shape, dt))

        def pb(name, shape, dt=F32):
            return ctx.enter_context(nc.psum_tensor(name, shape, dt))

        def sem(name):
            return ctx.enter_context(nc.semaphore(name))

        ident = sb("ident", [P, P])
        tri_f = sb("tri_f", [P, P])
        tri = sb("tri", [P, P], F32R)
        ones_r = sb("ones_r", [P, P], F32R)
        ones_f = sb("ones_f", [1, P])
        blockmask = sb("blockmask", [2 * NM, NM])
        minus_half = sb("minus_half", [P, SJ])
        plus_half = sb("plus_half", [P, SJ])
        w_in = sb("w_in", [P, 4, DIM])
        b_row = sb("b_row", [1, 4 * DIM])
        bias = sb("bias", [P, 4 * DIM])
        wqkv_hi = sb("wqkv_hi", [P, QKV], F32R)
        wqkv_lo = sb("wqkv_lo", [P, QKV], F32R)
        wo_t = sb("wo_t", [P, DIM])
        gx_col = sb("gx_col", [P, 1])
        gs_col = sb("gs_col", [P, 1])
        se_in = sb("se_in", [P, SJ, DIM])
        se_sq = sb("se_sq", [P, SJ, DIM])
        se_norm = sb("se_norm", [P, SJ])
        se_f = sb("se_f", [P, SLOTS])
        se_hi = sb("se_hi", [P, SLOTS], F32R)
        se_lo = sb("se_lo", [P, SLOTS], F32R)
        w1_in = sb("w1_in", [P, HID])
        w1_hi = sb("w1_hi", [P, HID], F32R)
        w1_lo = sb("w1_lo", [P, HID], F32R)
        w2_in = sb("w2_in", [P, FJ, DIM])

        X = [sb(f"X{u}", [P, NC, DIM]) for u in range(2)]
        xh = sb("xh", [P, NC, DIM])
        xT_hi = sb("xT_hi", [P, SEQ], F32R)
        xT_lo = sb("xT_lo", [P, SEQ], F32R)
        qkv = sb("qkv", [P, NC, QKV])
        Q = [sb(f"Q{u}", [P, NC, DIM]) for u in range(2)]
        kv = sb("kv", [P, NC, FEAT])
        kv_hi = [sb(f"kv_hi{u}", [P, NC, FEAT], F32R) for u in range(2)]
        kv_lo = [sb(f"kv_lo{u}", [P, NC, FEAT], F32R) for u in range(2)]
        prod = sb("prod", [P, NC, FEAT])
        numden = sb("numden", [P, NC, DIM + NH])
        den_inv = sb("den_inv", [P, NC, NH])
        att = sb("att", [P, NC, DIM])
        attT = sb("attT", [P, SEQ])
        y = sb("y", [P, NC, DIM])
        x1 = [sb(f"x1_{u}", [P, NC, DIM]) for u in range(2)]
        x1_res = [sb(f"x1_res{u}", [P, NC, DIM]) for u in range(2)]
        xn = [sb(f"xn{u}", [P, NC, XW]) for u in range(2)]

        xnT_hi = sb("xnT_hi", [P, SEQ], F32R)
        xnT_lo = sb("xnT_lo", [P, SEQ], F32R)
        maxima = sb("maxima", [P, NM])
        neg_max = sb("neg_max", [P, 2 * NM], F32R)
        max_rows = sb("max_rows", [2 * NM, NM, P], F32R)
        disp = sb("disp", [P, NC, SLOTS])
        comb = [sb(f"comb{u}", [P, SJ, SEQ]) for u in range(2)]
        disp_inv = sb("disp_inv", [P, SJ])
        slots = sb("slots", [P, SJ, DIM])
        slT_hi = sb("slT_hi", [P, SLOTS], F32R)
        slT_lo = sb("slT_lo", [P, SLOTS], F32R)
        hid = sb("hid", [P, FJ, SLOTS])
        proc = sb("proc", [P, SJ, XW])
        comb_inv = sb("comb_inv", [P, NC])
        mix = sb("mix", [P, NC, DIM])
        mixh = sb("mixh", [P, NC, DIM])
        res = [sb(f"res{u}", [P, NC, DIM]) for u in range(2)]

        def stats_set(name):
            return (sb(name + "_st", [P, NC, 6]), sb(name + "_mv", [P, NC, 2]), sb(name + "_ve", [P, NC]),
                    sb(name + "_rs", [P, NC]))

        st_x, st_y, st_1, st_o = (stats_set("ln_" + n) for n in ("x", "y", "x1", "mix"))
        root_v = sb("root_v", [P, NC])
        rms_n = sb("rms_n", [P, NC])
        rms_inv = sb("rms_inv", [P, NC])
        scale_n = sb("scale_n", [P, NC])

        WB = pb("WB", [P, 2, 512])
        LA = pb("LA", [P, 2, 512])
        LB = pb("LB", [P, 2, 512])
        HB = pb("HB", [P, 2, 512])
        LBv = LB[:, :, :].rearrange("p g (j t) -> p (g j) t", t=SEQ)
        SL = LA[:, :, 0:2 * XW].rearrange("p g (j d) -> p g j d", d=XW)
        OB = HB[:, 1, 0:NC * XW].rearrange("p (c d) -> p c d", d=XW)
        PR = HB[:, 0, :].rearrange("p (j d) -> p j d", d=DIM)

        s_const = sem("s_const")
        s_wload = sem("s_wload")
        s_seload = sem("s_seload")
        s_pe0 = sem("s_pe0")
        s_sesum = sem("s_sesum")
        s_senorm = sem("s_senorm")
        s_dve0 = sem("s_dve0")
        s_setup = sem("s_setup")
        s_dve0s = sem("s_dve0s")
        x_loaded = [sem(f"x_loaded{u}") for u in range(2)]
        x_stats, x_var, x_rstd, xh_ready, xT_done = (sem("s_" + n) for n in ("xst", "xve", "xrs", "xh", "xT"))
        xT_hi_ready, xT_lo_ready = sem("s_xThi"), sem("s_xTlo")
        qkv_done = [sem(f"s_qkv{c}") for c in range(NC)]
        biased = [sem(f"s_biased{c}") for c in range(NC)]
        q_ready, k_ready = sem("s_q"), sem("s_k")
        kv_built, kv_hi_ready, kv_lo_ready = sem("s_kv"), sem("s_kvhi"), sem("s_kvlo")
        UN = 2 * NC + 1
        cum_done = [sem(f"s_cum{k}") for k in range(UN)]
        prod_ready = [sem(f"s_prod{k}") for k in range(UN)]
        summed, den_ready, att_ready, att_T, attT_ready = (
            sem("s_" + n) for n in ("summed", "deninv", "att", "attTp", "attT"))
        wo_done, y_ready, y_stats, y_var, y_rstd, yh_ready, x1_ready = (
            sem("s_" + n) for n in ("wo", "y", "yst", "yve", "yrs", "yh", "x1"))
        x1_stats, x1_var, x1_rms, x1_inv, xn_ready, x1_saved = (
            sem("s_" + n) for n in ("x1st", "x1ve", "x1rms", "x1inv", "xn", "x1save"))
        x1_pool = sem("s_x1pool")
        xnT_done, xnT_hi_ready, xnT_lo_ready = sem("s_xnT"), sem("s_xnThi"), sem("s_xnTlo")
        la_done, lb_done, max_ready, neg_hi, neg_ready, maxT_done, rows_ready = (
            sem("s_" + n) for n in ("la", "lb", "max", "neghi", "neg", "maxT", "rows"))
        la_shifted, lb_shifted, disp_ready, comb_ready = (sem("s_" + n) for n in ("las", "lbs", "disp", "comb"))
        slots_done, slots_inv, slots_ready, slT_done, slT_hi_ready, slT_lo_ready = (
            sem("s_" + n) for n in ("sl", "slinv", "slots", "slT", "slThi", "slTlo"))
        hid_done = [sem(f"s_hid{f}") for f in range(FJ)]
        gelu_ready = [sem(f"s_gelu{f}") for f in range(FJ)]
        proc_done, proc_ready, mix_done, mix_inv, mix_ready, mix_stats, mix_var, mix_rstd, mixh_ready, res_ready = (
            sem("s_" + n) for n in ("proc", "procs", "mix", "mixinv", "mixs", "mixst", "mixve", "mixrs", "mixh", "res"))
        stored = [sem(f"stored{u}") for u in range(2)]

        def after(eng, s, n):
            if not isinstance(n, int) or 0 <= n < NB:
                eng.wait_ge(s, n + 1)

        def after_apart(eng, s, n):
            value = n + 1 if isinstance(n, int) else eng.to_reg(n + 1)
            eng.wait_ge(s_const, 8)
            eng.wait_ge(s, value)

        LOOP_FROM, LOOP_TO = 2, NB - 4

        def pipeline(eng, step):
            for s in range(-3, LOOP_FROM):
                rows = [(s + k, (s + k) % 2) if 0 <= s + k < NB else None for k in range(4)]
                step(*rows)
            with eng.Fori(LOOP_FROM // 2, LOOP_TO // 2) as m:
                for j in range(2):
                    step(*[(2 * m + (j + k), (j + k) % 2) for k in range(4)])
            for s in range(LOOP_TO, NB):
                rows = [(s + k, (s + k) % 2) if 0 <= s + k < NB else None for k in range(4)]
                step(*rows)

        block = ctx.enter_context(nc.Block())

        @block.sync
        def _(sp):
            for i, w in enumerate((wq, wk, wv, wo)):
                sp.dma_start(w_in[:, i, :], w).then_inc(s_wload, 16)
            for i, b in enumerate((bq, bk, bv, bo)):
                sp.dma_start(b_row[0:1, i * DIM:(i + 1) * DIM], b.rearrange("(a n) -> a n", a=1)).then_inc(s_wload, 16)
            for u in range(2):
                sp.dma_start(X[u][:, :, :], x_v[u]).then_inc(x_loaded[u], 16)
            sp.dma_start(gx_col[:, :], gamma_x.rearrange("(p a) -> p a", a=1)).then_inc(s_seload, 16)
            sp.dma_start(gs_col[:, :], gamma_slot.rearrange("(p a) -> p a", a=1)).then_inc(s_seload, 16)
            se_v = slot_embeds.rearrange("e t d -> (e t) d").rearrange("(j p) d -> p j d", p=P)
            sp.dma_start(se_in[:, :, :], se_v).then_inc(s_seload, 16)
            sp.dma_start(w1_in[:, :], w1).then_inc(s_seload, 16)
            sp.dma_start(w2_in[:, :, :], w2.rearrange("(j p) d -> p j d", p=P)).then_inc(s_seload, 16)

            def step(b, l, t, u3):
                if b:
                    n, u = b
                    after(sp, res_ready, n)
                    sp.dma_start(out_v[bass.ds(n, 1)].rearrange("b p c d -> p (b c) d") if not isinstance(n, int)
                                 else out_v[n], res[u][:, :, :]).then_inc(stored[u], 16)
                if t:
                    n, u = t
                    if isinstance(n, int) and n + 2 >= NB:
                        return
                    after(sp, x1_ready, n)
                    m = n + 2
                    sp.dma_start(X[u][:, :, :], x_v[bass.ds(m, 1)].rearrange("b p c d -> p (b c) d")
                                 if not isinstance(m, int) else x_v[m]).then_inc(x_loaded[u], 16)

            pipeline(sp, step)
            sp.wait_ge(stored[0], 16 * (NB // 2))
            sp.wait_ge(stored[1], 16 * (NB // 2))

        @block.gpsimd
        def _(pool):
            pool.memset(ident[:, :], 0.0).then_inc(s_const, 1)
            pool.memset(tri_f[:, :], 1.0).then_inc(s_const, 1)
            pool.memset(blockmask[:, :], 0.0).then_inc(s_const, 1)
            pool.memset(ones_r[:, :].bitcast(F32), 1.0)
            pool.memset(ones_f[:, :], 1.0)
            pool.memset(minus_half[:, :], -0.5)
            pool.memset(plus_half[:, :], 0.5)
            for u in range(2):
                pool.memset(xn[u][:, :, DIM:XW], 1.0)
            pool.memset(proc[:, :, DIM:XW], 1.0).then_inc(s_const, 1)
            pool.wait_ge(s_const, 4)
            pool.affine_select(out=ident[:, :], in_=ident[:, :], compare_op=ALU.not_equal, fill=1.0, base=0,
                               pattern=[[-1, P]], channel_multiplier=1).then_inc(s_const, 1)
            pool.affine_select(out=tri_f[:, :], in_=tri_f[:, :], compare_op=ALU.is_ge, fill=0.0, base=0,
                               pattern=[[1, P]], channel_multiplier=-1).then_inc(s_const, 1)
            pool.affine_select(out=blockmask[:, :], in_=blockmask[:, :], compare_op=ALU.not_equal, fill=1.0, base=0,
                               pattern=[[-1, NM]], channel_multiplier=1).then_inc(s_const, 1)
            pool.wait_ge(s_const, 7)
            pool.affine_select(out=blockmask[:, :], in_=blockmask[:, :], compare_op=ALU.not_equal, fill=1.0, base=-NM,
                               pattern=[[-1, NM]], channel_multiplier=1).then_inc(s_const, 1)
            pool.wait_ge(s_sesum, 1)
            pool.tensor_tensor(se_norm[:, :], se_norm[:, :], plus_half[:, :], ALU.pow).then_inc(s_senorm, 1)
            pool.wait_ge(s_senorm, 1)
            pool.tensor_scalar(se_norm[:, :], se_norm[:, :], EPS_RMS, 1.0, ALU.max, ALU.mult).then_inc(s_senorm, 1)

            def rstd(stats_done, var_done, rstd_done, st, n):
                _, mv, ve, rs = st
                after_apart(pool, stats_done, n)
                pool.tensor_scalar(ve[:, :], mv[:, :, 1], EPS_LN, 1.0, ALU.add, ALU.mult).then_inc(var_done, 1)
                after(pool, var_done, n)
                pool.tensor_tensor(rs[:, :], ve[:, :], minus_half[:, 0:NC], ALU.pow).then_inc(rstd_done, 1)

            def step(b, l, t, u3):
                if u3:
                    n, u = u3
                    rstd(x_stats, x_var, x_rstd, st_x, n)
                if l:
                    n, u = l
                    after_apart(pool, x1_ready, n)
                    after(pool, res_ready, n - 2)
                    pool.tensor_copy(x1_res[u][:, :, :], x1[u][:, :, :]).then_inc(x1_saved, 1)
                if u3:
                    n, u = u3
                    after(pool, k_ready, n)
                    after(pool, biased[NC - 1], n)
                    after(pool, kv_hi_ready, n - 1)
                    after(pool, kv_lo_ready, n - 1)
                    for c in range(NC):
                        k_b = kv[:, c, KVF:FEAT].rearrange("p (h o e) -> p h o e", h=NH, o=1).broadcast_to((P, NH, HD, HD))
                        v_b = qkv[:, c, 2 * DIM:QKV].rearrange("p (h d o) -> p h d o", h=NH, o=1)\
                            .broadcast_to((P, NH, HD, HD))
                        last = pool.tensor_tensor(kv[:, c, 0:KVF].rearrange("p (h d e) -> p h d e", h=NH, d=HD),
                                                  k_b, v_b, ALU.mult)
                    last.then_inc(kv_built, 1)
                if b:
                    n, u = b
                    rstd(mix_stats, mix_var, mix_rstd, st_o, n)
                if t:
                    n, u = t
                    rstd(y_stats, y_var, y_rstd, st_y, n)
                    rstd(x1_stats, x1_var, x1_rms, st_1, n)
                    mv, rs = st_1[1], st_1[3]
                    pool.tensor_scalar(root_v[:, :], mv[:, :, 1], float(DIM), 0.0, ALU.mult, ALU.add).then_inc(x1_pool, 1)
                    pool.wait_ge(x1_pool, 4 * n + 1)
                    pool.tensor_tensor(root_v[:, :], root_v[:, :], plus_half[:, 0:NC], ALU.pow).then_inc(x1_pool, 1)
                    after(pool, x1_rms, n)
                    pool.wait_ge(x1_pool, 4 * n + 2)
                    pool.tensor_tensor(rms_n[:, :], root_v[:, :], rs[:, :], ALU.mult).then_inc(x1_pool, 1)
                    after_apart(pool, x1_pool, 4 * n + 2)
                    pool.tensor_scalar(rms_n[:, :], rms_n[:, :], EPS_RMS, 1.0 / ROOT_DIM, ALU.max, ALU.mult)\
                        .then_inc(x1_pool, 1)

            pipeline(pool, step)

        @block.scalar
        def _(act):
            def copy(dst, src):
                return act.activation(dst, src, ACT.Copy)

            def step(b, l, t, u3):
                if b:
                    n, u = b
                    for f in range(FJ):
                        after(act, hid_done[f], n)
                        if f == 0:
                            after(act, proc_done, n - 1)
                        act.activation(hid[:, f, :], HB[:, f % 2, :], ACT.Gelu).then_inc(gelu_ready[f], 1)
                if u3:
                    n, u = u3
                    after(act, xT_done, n)
                    after(act, qkv_done[NC - 1], n - 1)
                    copy(xT_hi[:, :], WB[:, 0, 0:SEQ]).then_inc(xT_hi_ready, 1)
                if l:
                    n, u = l
                    after(act, xnT_done, n)
                    after(act, lb_done, n - 1)
                    copy(xnT_hi[:, :], WB[:, 1, 0:SEQ]).then_inc(xnT_hi_ready, 1)
                if u3:
                    n, u = u3
                    after(act, biased[NC - 1], n)
                    after(act, biased[0], n)
                    after(act, kv_hi_ready, n - 1)
                    after(act, kv_lo_ready, n - 1)
                    act.activation(kv[:, :, KVF:FEAT], qkv[:, :, DIM:2 * DIM], ACT.Exp).then_inc(k_ready, 1)
                    after(act, prod_ready[UN - 1], n - 2)
                    act.activation(Q[u][:, :, :], qkv[:, :, 0:DIM], ACT.Exp).then_inc(q_ready, 1)
                if b:
                    n, u = b
                    after(act, proc_done, n)
                    after(act, mix_done, n - 1)
                    copy(proc[:, :, 0:DIM], PR).then_inc(proc_ready, 1)
                if l:
                    n, u = l
                    after(act, la_shifted, n)
                    after(act, slots_done, n - 1)
                    for c in range(NC):
                        last = act.activation(disp[:, c, :], LA[:, c, :], ACT.Exp)
                    last.then_inc(disp_ready, 1)
                    after(act, lb_shifted, n)
                    after(act, mix_done, n - 2)
                    for g in range(2):
                        last = act.activation(comb[u][:, 2 * g:2 * g + 2, :], LBv[:, 2 * g:2 * g + 2, :], ACT.Exp)
                    last.then_inc(comb_ready, 1)
                if u3:
                    n, u = u3
                    after(act, kv_built, n)
                    after(act, k_ready, n)
                    after(act, cum_done[UN - 1], n - 2)
                    copy(kv_hi[u][:, :, :], kv[:, :, :]).then_inc(kv_hi_ready, 1)
                if l:
                    n, u = l
                    after(act, slT_done, n)
                    after(act, hid_done[FJ - 1], n - 1)
                    copy(slT_hi[:, :], LB[:, 0, :]).then_inc(slT_hi_ready, 1)
                if t:
                    n, u = t
                    after(act, att_T, n)
                    after(act, wo_done, n - 1)
                    copy(attT[:, :], WB[:, 0, 0:SEQ]).then_inc(attT_ready, 1)

            pipeline(act, step)

        @block.tensor
        def _(pe):
            pe.wait_ge(s_const, 8)
            pe.wait_ge(s_wload, 16 * 8)
            for i in range(4):
                last = pe.transpose(WB[:, 0, i * P:(i + 1) * P], w_in[:, i, :], ident[:, :])
            last.then_inc(s_pe0, 1)
            pe.matmul(WB[:, 1, :], ones_f[0:1, :], b_row[0:1, :], start=True, stop=True).then_inc(s_pe0, 1)
            pe.wait_ge(s_dve0, 1)
            for j in range(SJ):
                last = pe.transpose(LA[:, 0, j * P:(j + 1) * P], se_in[:, j, :], ident[:, :])
            last.then_inc(s_pe0, 1)
            pe.wait_ge(s_setup, 1)

            def three(dst, a_hi, a_lo, b_hi, b_lo, start=True, stop=True):
                pe.matmul(dst, a_hi, b_hi, start=start, stop=False, skip_group_check=True)
                pe.matmul(dst, a_hi, b_lo, start=False, stop=False, skip_group_check=True)
                return pe.matmul(dst, a_lo, b_hi, start=False, stop=stop, skip_group_check=True)

            def hidden(n, u):
                after(pe, slT_hi_ready, n)
                after(pe, slT_lo_ready, n)
                for f in range(FJ):
                    if f == 0:
                        after(pe, proc_ready, n - 1)
                    elif f == 1:
                        after(pe, mix_ready, n - 1)
                    else:
                        after(pe, gelu_ready[f - 2], n)
                    cols = slice(f * P, (f + 1) * P)
                    three(HB[:, f % 2, :], w1_hi[:, cols], w1_lo[:, cols], slT_hi[:, :], slT_lo[:, :])\
                        .then_inc(hid_done[f], 1)

            def x_transpose(n, u):
                after(pe, xh_ready, n)
                after(pe, attT_ready, n - 2)
                after(pe, biased[0], n - 1)
                for c in range(NC):
                    last = pe.transpose(WB[:, 0, c * P:(c + 1) * P], xh[:, c, :], ident[:, :])
                last.then_inc(xT_done, 1)

            def xn_transpose(n, u):
                after(pe, xn_ready, n)
                after(pe, biased[NC - 1], n + 1)
                for c in range(NC):
                    last = pe.transpose(WB[:, 1, c * P:(c + 1) * P], xn[u][:, c, 0:DIM], ident[:, :])
                last.then_inc(xnT_done, 1)

            def project(n, u, l):
                after(pe, xT_hi_ready, n)
                after(pe, xT_lo_ready, n)
                for c in range(NC):
                    if c == 1:
                        after(pe, xnT_hi_ready, n - 2)
                        after(pe, xnT_lo_ready, n - 2)
                        after(pe, biased[1], n - 1)
                    cols = slice(c * P, (c + 1) * P)
                    three(WB[:, c, 0:QKV], xT_hi[:, cols], xT_lo[:, cols], wqkv_hi[:, :], wqkv_lo[:, :])\
                        .then_inc(qkv_done[c], 1)

            def logits(n, u):
                after(pe, xnT_hi_ready, n)
                after(pe, xnT_lo_ready, n)
                after(pe, slots_ready, n - 1)
                after(pe, slT_hi_ready, n - 1)
                after(pe, slT_lo_ready, n - 1)
                for c in range(NC):
                    cols = slice(c * P, (c + 1) * P)
                    last = three(LA[:, c, :], xnT_hi[:, cols], xnT_lo[:, cols], se_hi[:, :], se_lo[:, :], stop=False)
                last.then_inc(la_done, 1)
                for j in range(SJ):
                    cols = slice(j * P, (j + 1) * P)
                    last = three(LBv[:, j, :], se_hi[:, cols], se_lo[:, cols], xnT_hi[:, :], xnT_lo[:, :],
                                 start=(j % 2 == 0), stop=False)
                last.then_inc(lb_done, 1)

            def max_transpose(n, u, u3):
                after(pe, neg_ready, n)
                after(pe, biased[0], n + 2)
                pe.transpose(WB[0:2 * NM, 0, 0:P], neg_max[:, :].bitcast(F32), ident[:, :]).then_inc(maxT_done, 1)

            def subtract_max(n, u):
                after(pe, rows_ready, n)
                rows_f = max_rows[:, :, :].rearrange("p m t -> p (m t)")
                for c in range(NC):
                    last = pe.matmul(LA[:, c, :], ones_r[0:2 * NM, :], rows_f[:, 0:SLOTS], start=False, stop=True,
                                     skip_group_check=True)
                last.then_inc(la_shifted, 1)
                for j in range(SJ):
                    last = pe.matmul(LBv[:, j, :], ones_r[0:2 * NM, :], rows_f[:, SLOTS:SLOTS + SEQ], start=False,
                                     stop=True, skip_group_check=True)
                last.then_inc(lb_shifted, 1)

            def cumulate(n, u, k):
                if k == 0:
                    after(pe, kv_hi_ready, n)
                    after(pe, kv_lo_ready, n)
                    after(pe, biased[1], n + 1)
                elif k == 1:
                    after(pe, rows_ready, n - 1)
                    after(pe, biased[0], n + 1)
                else:
                    after(pe, prod_ready[k - 2], n)
                bank = (k + 1) % 2
                if k < 2 * NC:
                    c, f = k // 2, slice((k % 2) * HALF, (k % 2 + 1) * HALF)
                    tiles = [(c, WB[:, bank, 0:HALF], f)]
                else:
                    tiles = [(c, WB[:, bank, c * DIM:(c + 1) * DIM], slice(KVF, FEAT)) for c in range(NC)]
                for c, dst, f in tiles:
                    terms = [(ones_r, a[u][:, e, f]) for e in range(c) for a in (kv_hi, kv_lo)]
                    terms += [(tri, a[u][:, c, f]) for a in (kv_hi, kv_lo)]
                    for i, (m, a) in enumerate(terms):
                        last = pe.matmul(dst, m[:, :], a, start=(i == 0), stop=(i == len(terms) - 1))
                last.then_inc(cum_done[k], 1)

            def att_transpose(n, u):
                after(pe, att_ready, n)
                for c in range(NC):
                    last = pe.transpose(WB[:, 0, c * P:(c + 1) * P], att[:, c, :], ident[:, :])
                last.then_inc(att_T, 1)

            def attention_out(n, u):
                after(pe, attT_ready, n)
                for c in range(NC):
                    last = pe.matmul(WB[:, 1, c * DIM:(c + 1) * DIM], attT[:, c * P:(c + 1) * P], wo_t[:, :],
                                     start=True, stop=True)
                last.then_inc(wo_done, 1)

            def gather_slots(n, u):
                after(pe, disp_ready, n)
                for j in range(SJ):
                    for c in range(NC):
                        last = pe.matmul(SL[:, j // 2, j % 2, 0:DIM + 1], disp[:, c, j * P:(j + 1) * P],
                                         xn[u][:, c, 0:DIM + 1], start=(c == 0), stop=(c == NC - 1))
                last.then_inc(slots_done, 1)

            def slots_transpose(n, u):
                after(pe, slots_ready, n)
                after(pe, comb_ready, n)
                for j in range(SJ):
                    last = pe.transpose(LB[:, 0, j * P:(j + 1) * P], slots[:, j, :], ident[:, :])
                last.then_inc(slT_done, 1)

            def process(n, u):
                for f in range(FJ):
                    after(pe, gelu_ready[f], n)
                for j in range(SJ):
                    for f in range(FJ):
                        last = pe.matmul(PR[:, j, :], hid[:, f, j * P:(j + 1) * P], w2_in[:, f, :],
                                         start=(f == 0), stop=(f == FJ - 1))
                last.then_inc(proc_done, 1)

            def mixture(n, u):
                after(pe, proc_ready, n)
                after(pe, comb_ready, n)
                for c in range(NC):
                    for j in range(SJ):
                        last = pe.matmul(OB[:, c, 0:DIM + 1], comb[u][:, j, c * P:(c + 1) * P],
                                         proc[:, j, 0:DIM + 1], start=(j == 0), stop=(j == SJ - 1))
                last.then_inc(mix_done, 1)

            def step(b, l, t, u3):
                if b:
                    hidden(*b)
                if u3:
                    x_transpose(*u3)
                if l:
                    xn_transpose_early = l
                    after(pe, xn_ready, l[0])
                    for c in range(NC):
                        last = pe.transpose(WB[:, 1, c * P:(c + 1) * P], xn[l[1]][:, c, 0:DIM], ident[:, :])
                    last.then_inc(xnT_done, 1)
                if u3:
                    project(u3[0], u3[1], l)
                if l:
                    logits(*l)
                if t:
                    cumulate(*t, 0)
                if b:
                    process(*b)
                if l:
                    max_transpose(l[0], l[1], u3)
                if t:
                    cumulate(*t, 1)
                if l:
                    subtract_max(*l)
                if t:
                    cumulate(*t, 2)
                    cumulate(*t, 3)
                    cumulate(*t, 4)
                if l:
                    gather_slots(*l)
                if b:
                    mixture(*b)
                if l:
                    slots_transpose(*l)
                if t:
                    att_transpose(*t)
                    attention_out(*t)

            pipeline(pe, step)

        @block.vector
        def _(dve):
            dve.wait_ge(s_const, 8)
            dve.tensor_copy(tri[:, :], tri_f[:, :])
            dve.wait_ge(s_seload, 16 * 5)
            dve.tensor_tensor(se_sq[:, :, :], se_in[:, :, :], se_in[:, :, :], ALU.mult).then_inc(s_dve0s, 1)
            dve.wait_ge(s_dve0s, 1)
            dve.tensor_reduce(se_norm[:, :], se_sq[:, :, :], AX.X, ALU.add).then_inc(s_sesum, 1)
            dve.tensor_scalar(w1_in[:, :], w1_in[:, :], gx_col[:, 0:1], None, ALU.mult).then_inc(s_dve0s, 1)
            dve.wait_ge(s_dve0s, 2)
            dve.tensor_copy(w1_hi[:, :], w1_in[:, :]).then_inc(s_dve0s, 1)
            dve.wait_ge(s_dve0s, 3)
            dve.tensor_tensor(w1_lo[:, :], w1_in[:, :], w1_hi[:, :].bitcast(F32), ALU.subtract)
            dve.wait_ge(s_senorm, 2)
            dve.reciprocal(se_norm[:, :], se_norm[:, :]).then_inc(s_dve0s, 1)
            dve.wait_ge(s_dve0s, 4)
            dve.tensor_scalar(se_norm[:, :], se_norm[:, :], ROOT_DIM, None, ALU.mult).then_inc(s_dve0s, 1)
            dve.wait_ge(s_dve0s, 5)
            dve.tensor_tensor(se_in[:, :, :], se_in[:, :, :],
                              se_norm[:, :].rearrange("p (j o) -> p j o", o=1).broadcast_to((P, SJ, DIM)),
                              ALU.mult).then_inc(s_dve0, 1)
            dve.wait_ge(s_pe0, 1)
            dve.tensor_copy(wqkv_hi[:, :], WB[:, 0, 0:QKV]).then_inc(s_dve0s, 1)
            dve.tensor_copy(wo_t[:, :], WB[:, 0, QKV:QKV + DIM])
            dve.wait_ge(s_dve0s, 6)
            dve.tensor_tensor(wqkv_lo[:, :], WB[:, 0, 0:QKV], wqkv_hi[:, :].bitcast(F32), ALU.subtract)
            dve.wait_ge(s_pe0, 2)
            dve.tensor_copy(bias[:, :], WB[:, 1, :]).then_inc(s_dve0s, 1)
            dve.wait_ge(s_pe0, 3)
            dve.tensor_scalar(se_f[:, :], LA[:, 0, :], gx_col[:, 0:1], gs_col[:, 0:1], ALU.mult, ALU.mult)\
                .then_inc(s_dve0s, 1)
            dve.wait_ge(s_dve0s, 8)
            dve.tensor_copy(se_hi[:, :], se_f[:, :]).then_inc(s_dve0s, 1)
            dve.wait_ge(s_dve0s, 9)
            dve.tensor_tensor(se_lo[:, :], se_f[:, :], se_hi[:, :].bitcast(F32), ALU.subtract).then_inc(s_setup, 1)

            def low_part(dst, a, hi):
                return dve.tensor_tensor(dst, a, hi.bitcast(F32), ALU.subtract)

            def stats(st, src, ready, done, n, chain):
                s6, mv = st[0], st[1]
                after(dve, ready, n)
                for c in range(NC):
                    last = dve.bn_stats(s6[:, c, :], src[:, c, :])
                last.then_inc(chain, 1)
                after_apart(dve, chain, n)
                for c in range(NC):
                    last = dve.bn_aggr(mv[:, c, :], s6[:, c, :])
                last.then_inc(done, 1)

            x_chain, y_chain, x1_chain, mix_chain = (sem("s_ch" + n) for n in ("x", "y", "x1", "mix"))

            def normalise(dst, src, st, done):
                mv, rs = st[1], st[3]
                for c in range(NC):
                    last = dve.tensor_scalar(dst[:, c, :], src[:, c, :], mv[:, c, 0:1], rs[:, c:c + 1],
                                             ALU.subtract, ALU.mult)
                last.then_inc(done, 1)

            def x_stat(n, u, half):
                s6, mv = st_x[0], st_x[1]
                dve.wait_ge(x_loaded[u], 16 * half)
                after(dve, xh_ready, n - 1)
                for c in range(NC):
                    last = dve.bn_stats(s6[:, c, :], X[u][:, c, :])
                last.then_inc(x_chain, 1)
                after_apart(dve, x_chain, n)
                for c in range(NC):
                    last = dve.bn_aggr(mv[:, c, :], s6[:, c, :])
                last.then_inc(x_stats, 1)

            def x_norm(n, u):
                after(dve, x_rstd, n)
                after(dve, xT_done, n - 1)
                normalise(xh, X[u], st_x, xh_ready)

            def multiply(n, u, k):
                after(dve, cum_done[k], n)
                bank = (k + 1) % 2
                if k < 2 * NC:
                    c, g = k // 2, k % 2
                    q_b = Q[u][:, c, g * HH * HD:(g + 1) * HH * HD].rearrange("p (h o e) -> p h o e", h=HH, o=1)\
                        .broadcast_to((P, HH, HD, HD))
                    dve.tensor_tensor(prod[:, c, g * HALF:(g + 1) * HALF].rearrange("p (h d e) -> p h d e", h=HH, d=HD),
                                      WB[:, bank, 0:HALF].rearrange("p (h d e) -> p h d e", h=HH, d=HD),
                                      q_b, ALU.mult).then_inc(prod_ready[k], 1)
                else:
                    dve.tensor_tensor(prod[:, :, KVF:FEAT], WB[:, bank, 0:NC * DIM].rearrange("p (c d) -> p c d", c=NC),
                                      Q[u][:, :, :], ALU.mult).then_inc(prod_ready[k], 1)

            def step(b, l, t, u3):
                if u3:
                    n, u = u3
                    x_norm(n, u)
                    after(dve, xT_hi_ready, n)
                    after(dve, qkv_done[NC - 1], n - 1)
                    low_part(xT_lo[:, :], WB[:, 0, 0:SEQ], xT_hi[:, :]).then_inc(xT_lo_ready, 1)
                if l:
                    n, u = l
                    after(dve, xnT_hi_ready, n)
                    after(dve, lb_done, n - 1)
                    low_part(xnT_lo[:, :], WB[:, 1, 0:SEQ], xnT_hi[:, :]).then_inc(xnT_lo_ready, 1)
                if u3:
                    n, u = u3
                    after(dve, kv_built, n - 1)
                    after(dve, q_ready, n - 1)
                    for c in range(NC):
                        after(dve, qkv_done[c], n)
                        dve.tensor_tensor(qkv[:, c, :], WB[:, c, 0:QKV], bias[:, 0:QKV], ALU.add)\
                            .then_inc(biased[c], 1)
                if l:
                    n, u = l
                    after(dve, la_done, n)
                    after(dve, neg_ready, n - 1)
                    dve.tensor_reduce(maxima[:, SJ:NM], LA[:, :, :], AX.X, ALU.max)
                    after(dve, lb_done, n)
                    dve.tensor_reduce(maxima[:, 0:SJ], LBv, AX.X, ALU.max).then_inc(max_ready, 1)
                    after(dve, max_ready, n)
                    after(dve, maxT_done, n - 1)
                    dve.tensor_scalar(neg_max[:, 0:NM], maxima[:, :], -1.0, None, ALU.mult).then_inc(neg_hi, 1)
                    after(dve, neg_hi, n)
                    dve.scalar_tensor_tensor(out=neg_max[:, NM:2 * NM], in0=maxima[:, :], scalar=-1.0,
                                             in1=neg_max[:, 0:NM].bitcast(F32), op0=ALU.mult, op1=ALU.subtract)\
                        .then_inc(neg_ready, 1)
                if t:
                    n, u = t
                    after(dve, q_ready, n)
                    after(dve, summed, n - 1)
                    multiply(n, u, 0)
                if l:
                    n, u = l
                    after(dve, maxT_done, n)
                    after(dve, lb_shifted, n - 1)
                    dve.tensor_tensor(max_rows[:, :, :],
                                      WB[0:2 * NM, 0, 0:P].rearrange("p (o t) -> p o t", o=1).broadcast_to((2 * NM, NM, P)),
                                      blockmask[:, :].rearrange("p (m o) -> p m o", o=1).broadcast_to((2 * NM, NM, P)),
                                      ALU.mult).then_inc(rows_ready, 1)
                if t:
                    n, u = t
                    for k in range(1, UN):
                        multiply(n, u, k)
                    for k in range(UN):
                        after(dve, prod_ready[k], n)
                    dve.tensor_reduce(numden[:, :, :], prod[:, :, :].rearrange("p c (f e) -> p c f e", e=HD),
                                      AX.X, ALU.add).then_inc(summed, 1)
                    after(dve, summed, n)
                    dve.reciprocal(den_inv[:, :, :], numden[:, :, DIM:DIM + NH]).then_inc(den_ready, 1)
                    after(dve, den_ready, n)
                    after(dve, att_T, n - 1)
                    dve.tensor_tensor(att[:, :, :].rearrange("p c (h d) -> p c h d", h=NH),
                                      numden[:, :, 0:DIM].rearrange("p c (h d) -> p c h d", h=NH),
                                      den_inv[:, :, :].rearrange("p c (h o) -> p c h o", o=1)
                                      .broadcast_to((P, NC, NH, HD)), ALU.mult).then_inc(att_ready, 1)
                if l:
                    n, u = l
                    after(dve, slots_done, n)
                    dve.reciprocal(disp_inv[:, :].rearrange("p (g j) -> p g j", g=2), SL[:, :, :, DIM])\
                        .then_inc(slots_inv, 1)
                    after(dve, slots_inv, n)
                    after(dve, slT_done, n - 1)
                    dve.tensor_tensor(slots[:, :, :].rearrange("p (g j) d -> p g j d", g=2), SL[:, :, :, 0:DIM],
                                      disp_inv[:, :].rearrange("p (g j o) -> p g j o", g=2, o=1)
                                      .broadcast_to((P, 2, 2, DIM)), ALU.mult).then_inc(slots_ready, 1)
                if u3:
                    n, u = u3
                    after(dve, kv_hi_ready, n)
                    after(dve, cum_done[UN - 1], n - 2)
                    low_part(kv_lo[u][:, :, :], kv[:, :, :], kv_hi[u][:, :, :]).then_inc(kv_lo_ready, 1)
                if b:
                    n, u = b
                    after(dve, mix_done, n)
                    dve.reciprocal(comb_inv[:, :], OB[:, :, DIM]).then_inc(mix_inv, 1)
                    after(dve, mix_inv, n)
                    dve.tensor_tensor(mix[:, :, :], OB[:, :, 0:DIM],
                                      comb_inv[:, :].rearrange("p (c o) -> p c o", o=1).broadcast_to((P, NC, DIM)),
                                      ALU.mult).then_inc(mix_ready, 1)
                    stats(st_o, mix, mix_ready, mix_stats, n, mix_chain)
                if l:
                    n, u = l
                    after(dve, slT_hi_ready, n)
                    after(dve, hid_done[FJ - 1], n - 1)
                    low_part(slT_lo[:, :], LB[:, 0, :], slT_hi[:, :]).then_inc(slT_lo_ready, 1)
                if t:
                    n, u = t
                    after(dve, wo_done, n)
                    dve.tensor_tensor(y[:, :, :], WB[:, 1, 0:NC * DIM].rearrange("p (c d) -> p c d", c=NC),
                                      bias[:, QKV:QKV + DIM].rearrange("p (o d) -> p o d", o=1)
                                      .broadcast_to((P, NC, DIM)), ALU.add).then_inc(y_ready, 1)
                    stats(st_y, y, y_ready, y_stats, n, y_chain)
                if b:
                    n, u = b
                    after(dve, mix_rstd, n)
                    normalise(mixh, mix, st_o, mixh_ready)
                    after(dve, mixh_ready, n)
                    after(dve, x1_saved, n)
                    if not isinstance(n, int):
                        dve.wait_ge(stored[u], 8 * (n - u))
                    elif n >= 2:
                        dve.wait_ge(stored[u], 16 * (n // 2))
                    dve.tensor_tensor(res[u][:, :, :], mixh[:, :, :], x1_res[u][:, :, :], ALU.add)\
                        .then_inc(res_ready, 1)
                if t:
                    n, u = t
                    after(dve, y_rstd, n)
                    normalise(y, y, st_y, yh_ready)
                    after(dve, yh_ready, n)
                    after(dve, x1_saved, n - 2)
                    after(dve, xn_ready, n - 2)
                    dve.tensor_tensor(x1[u][:, :, :], y[:, :, :], X[u][:, :, :], ALU.add).then_inc(x1_ready, 1)
                    stats(st_1, x1[u], x1_ready, x1_stats, n, x1_chain)
                if u3:
                    nxt = u3[0] + 1
                    if not isinstance(nxt, int) or nxt < NB:
                        half = (nxt // 2 + 1) if isinstance(nxt, int) else None
                        uu = 1 - u3[1]
                        s6, mv = st_x[0], st_x[1]
                        if half is not None:
                            dve.wait_ge(x_loaded[uu], 16 * half)
                        else:
                            dve.wait_ge(x_loaded[uu], 8 * (nxt - uu + 2))
                        for c in range(NC):
                            last = dve.bn_stats(s6[:, c, :], X[uu][:, c, :])
                        last.then_inc(x_chain, 1)
                        after_apart(dve, x_chain, nxt)
                        for c in range(NC):
                            last = dve.bn_aggr(mv[:, c, :], s6[:, c, :])
                        last.then_inc(x_stats, 1)
                if t:
                    n, u = t
                    dve.wait_ge(x1_pool, 4 * n + 4)
                    dve.reciprocal(rms_inv[:, :], rms_n[:, :]).then_inc(x1_inv, 1)
                    after(dve, x1_inv, n)
                    after(dve, x1_rms, n)
                    dve.tensor_tensor(scale_n[:, :], rms_inv[:, :], st_1[3][:, :], ALU.mult).then_inc(x1_scale, 1)
                    after(dve, x1_scale, n)
                    for c in range(NC):
                        last = dve.tensor_scalar(xn[u][:, c, 0:DIM], x1[u][:, c, :], st_1[1][:, c, 0:1],
                                                 scale_n[:, c:c + 1], ALU.subtract, ALU.mult)
                    last.then_inc(xn_ready, 1)

            x1_scale = sem("s_x1scale")
            dve.wait_ge(x_loaded[0], 16)
            for c in range(NC):
                last = dve.bn_stats(st_x[0][:, c, :], X[0][:, c, :])
            last.then_inc(x_chain, 1)
            dve.wait_ge(x_chain, 1)
            for c in range(NC):
                last = dve.bn_aggr(st_x[1][:, c, :], st_x[0][:, c, :])
            last.then_inc(x_stats, 1)
            pipeline(dve, step)


_INS = ["L0_attn_x", "L0_attn_Wq", "L0_attn_bq", "L0_attn_Wk", "L0_attn_bk", "L0_attn_Wv", "L0_attn_bv",
        "L0_attn_Wo", "L0_attn_bo", "L0_ffn_gamma_x", "L0_ffn_gamma_slot", "L0_ffn_slot_embeds",
        "L0_ffn_w1", "L0_ffn_w2"]


def kernel(**inputs):
    import numpy as _np
    import concourse.bacc as _bacc
    from concourse import mybir as _mybir
    from concourse.bass_utils import run_bass_kernel_spmd as _run

    nc = _bacc.Bacc("TRN2", target_bir_lowering=False, num_devices=1)
    arrays, args = {}, []
    for name in _INS:
        a = _np.ascontiguousarray(inputs[name])
        arrays[f"in_{name}_dram"] = a
        args.append(nc.dram_tensor(f"in_{name}_dram", a.shape, _mybir.dt.from_np(a.dtype), kind="ExternalInput").ap())
    shape = inputs["L0_attn_x"].shape
    args.append(nc.dram_tensor("out_0_dram", shape, _mybir.dt.float32, kind="ExternalOutput").ap())
    attention_and_slot_mixture(nc, *args)
    r = _run(nc, [arrays], core_ids=[0])
    return r.results[0]["out_0_dram"]
```

```python
import concourse.bass as bass
from concourse import mybir
from contextlib import ExitStack


def attention_and_slot_mixture(
    nc: bass.Bass,
    x: bass.AP, wq: bass.AP, bq: bass.AP, wk: bass.AP, bk: bass.AP, wv: bass.AP, bv: bass.AP,
    wo: bass.AP, bo: bass.AP, gamma_x: bass.AP, gamma_slot: bass.AP, slot_embeds: bass.AP,
    w1: bass.AP, w2: bass.AP, out: bass.AP,
):
    F32 = mybir.dt.float32
    F32R = mybir.dt.float32r
    ALU = mybir.AluOpType
    ACT = mybir.ActivationFunctionType
    AX = mybir.AxisListType

    NB, SEQ, DIM = x.shape
    P = 128
    NC = SEQ // P
    NH = 16
    HD = DIM // NH
    NE, NT, _ = slot_embeds.shape
    SLOTS = NE * NT
    SJ = SLOTS // P
    HID = w1.shape[1]
    FJ = HID // P
    KVF = NH * HD * HD
    FEAT = KVF + DIM
    HALF = KVF // 2
    HH = NH // 2
    QKV = 3 * DIM
    XW = DIM + 2
    NM = SJ + NC
    EPS_LN = 1e-5
    EPS_RMS = 1e-12
    ROOT_DIM = float(DIM) ** 0.5

    x_v = x.rearrange("b (c p) d -> b p c d", p=P)
    out_v = out.rearrange("b (c p) d -> b p c d", p=P)

    ctx = ExitStack()
    with ctx:
        def sb(name, shape, dt=F32):
            return ctx.enter_context(nc.sbuf_tensor(name, shape, dt))

        def pb(name, shape, dt=F32):
            return ctx.enter_context(nc.psum_tensor(name, shape, dt))

        def sem(name):
            return ctx.enter_context(nc.semaphore(name))

        ident = sb("ident", [P, P])
        tri_f = sb("tri_f", [P, P])
        tri = sb("tri", [P, P], F32R)
        ones_r = sb("ones_r", [P, P], F32R)
        ones_f = sb("ones_f", [1, P])
        blockmask = sb("blockmask", [2 * NM, NM])
        minus_half = sb("minus_half", [P, SJ])
        plus_half = sb("plus_half", [P, SJ])
        w_in = sb("w_in", [P, 4, DIM])
        b_row = sb("b_row", [1, 4 * DIM])
        bias = sb("bias", [P, 4 * DIM])
        wqkv_hi = sb("wqkv_hi", [P, QKV], F32R)
        wqkv_lo = sb("wqkv_lo", [P, QKV], F32R)
        wo_t = sb("wo_t", [P, DIM])
        gx_col = sb("gx_col", [P, 1])
        gs_col = sb("gs_col", [P, 1])
        se_in = sb("se_in", [P, SJ, DIM])
        se_sq = sb("se_sq", [P, SJ, DIM])
        se_norm = sb("se_norm", [P, SJ])
        se_f = sb("se_f", [P, SLOTS])
        se_hi = sb("se_hi", [P, SLOTS], F32R)
        se_lo = sb("se_lo", [P, SLOTS], F32R)
        w1_in = sb("w1_in", [P, HID])
        w1_hi = sb("w1_hi", [P, HID], F32R)
        w1_lo = sb("w1_lo", [P, HID], F32R)
        w2_in = sb("w2_in", [P, FJ, DIM])

        X = [sb(f"X{u}", [P, NC, DIM]) for u in range(2)]
        xh = sb("xh", [P, NC, DIM])
        xT_hi = sb("xT_hi", [P, SEQ], F32R)
        xT_lo = sb("xT_lo", [P, SEQ], F32R)
        qkv = sb("qkv", [P, NC, QKV])
        Q = [sb(f"Q{u}", [P, NC, DIM]) for u in range(2)]
        kv = sb("kv", [P, NC, FEAT])
        kv_hi = sb("kv_hi", [P, NC, FEAT], F32R)
        kv_lo = sb("kv_lo", [P, NC, FEAT], F32R)
        x_res = [sb(f"x_res{u}", [P, NC, DIM]) for u in range(2)]
        prod = sb("prod", [P, NC, FEAT])
        numden = sb("numden", [P, NC, DIM + NH])
        den_inv = sb("den_inv", [P, NC, NH])
        att = sb("att", [P, NC, DIM])
        attT = sb("attT", [P, SEQ])
        y = sb("y", [P, NC, DIM])
        x1 = [sb(f"x1_{u}", [P, NC, DIM]) for u in range(2)]
        x1_res = [sb(f"x1_res{u}", [P, NC, DIM]) for u in range(2)]
        xn = [sb(f"xn{u}", [P, NC, XW]) for u in range(2)]

        xnT_hi = sb("xnT_hi", [P, SEQ], F32R)
        xnT_lo = sb("xnT_lo", [P, SEQ], F32R)
        maxima = sb("maxima", [P, NM])
        neg_max = sb("neg_max", [P, 2 * NM], F32R)
        max_rows = sb("max_rows", [2 * NM, NM, P], F32R)
        disp = sb("disp", [P, NC, SLOTS])
        comb = [sb(f"comb{u}", [P, SJ, SEQ]) for u in range(2)]
        disp_inv = sb("disp_inv", [P, SJ])
        slots = sb("slots", [P, SJ, DIM])
        slT_hi = sb("slT_hi", [P, SLOTS], F32R)
        slT_lo = sb("slT_lo", [P, SLOTS], F32R)
        hid = sb("hid", [P, FJ, SLOTS])
        proc = sb("proc", [P, SJ, XW])
        comb_inv = sb("comb_inv", [P, NC])
        mix = sb("mix", [P, NC, DIM])
        mixh = sb("mixh", [P, NC, DIM])
        res = [sb(f"res{u}", [P, NC, DIM]) for u in range(2)]

        def stats_set(name):
            return (sb(name + "_st", [P, NC, 6]), sb(name + "_mv", [P, NC, 2]), sb(name + "_ve", [P, NC]),
                    sb(name + "_rs", [P, NC]))

        st_x, st_y, st_1, st_o = (stats_set("ln_" + n) for n in ("x", "y", "x1", "mix"))
        neg_mean = sb("neg_mean", [P, NC])
        shift_x = sb("shift_x", [P, NC])
        shift_o = sb("shift_o", [P, NC])
        root_v = sb("root_v", [P, NC])
        rms_n = sb("rms_n", [P, NC])
        rms_inv = sb("rms_inv", [P, NC])
        rms_n2 = sb("rms_n2", [P, NC])
        scale_n = sb("scale_n", [P, NC])

        WB = pb("WB", [P, 2, 512])
        LA = pb("LA", [P, 2, 512])
        LB = pb("LB", [P, 2, 512])
        HB = pb("HB", [P, 2, 512])
        LBv = LB[:, :, :].rearrange("p g (j t) -> p (g j) t", t=SEQ)
        SL = LA[:, :, 0:2 * XW].rearrange("p g (j d) -> p g j d", d=XW)
        OB = HB[:, 1, 0:NC * XW].rearrange("p (c d) -> p c d", d=XW)
        PR = HB[:, 0, :].rearrange("p (j d) -> p j d", d=DIM)

        s_const = sem("s_const")
        s_wload = sem("s_wload")
        s_seload = sem("s_seload")
        s_pe0 = sem("s_pe0")
        s_sesum = sem("s_sesum")
        s_senorm = sem("s_senorm")
        s_dve0 = sem("s_dve0")
        s_setup = sem("s_setup")
        s_dve0s = sem("s_dve0s")
        x_loaded = [sem(f"x_loaded{u}") for u in range(2)]
        x_res_loaded = [sem(f"x_res_loaded{u}") for u in range(2)]
        x_stats, x_var, x_rstd, xh_ready, xT_done = (sem("s_" + n) for n in ("xst", "xve", "xrs", "xh", "xT"))
        xT_hi_ready, xT_lo_ready = sem("s_xThi"), sem("s_xTlo")
        qkv_done = [sem(f"s_qkv{c}") for c in range(NC)]
        biased = [sem(f"s_biased{c}") for c in range(NC)]
        q_ready, k_ready = sem("s_q"), sem("s_k")
        kv_built = sem("s_kv")
        kv_hi_ready = [sem(f"s_kvhi{c}") for c in range(NC)]
        kv_lo_ready = [sem(f"s_kvlo{c}") for c in range(NC)]
        UN = 2 * NC + 1
        cum_done = [sem(f"s_cum{k}") for k in range(UN)]
        prod_ready = [sem(f"s_prod{k}") for k in range(UN)]
        summed, den_ready, att_ready, att_T, attT_ready = (
            sem("s_" + n) for n in ("summed", "deninv", "att", "attTp", "attT"))
        wo_done, y_ready, y_stats, y_var, y_rstd, yh_ready, x1_ready = (
            sem("s_" + n) for n in ("wo", "y", "yst", "yve", "yrs", "yh", "x1"))
        x1_stats, x1_var, x1_rms, x1_inv, xn_ready, x1_saved = (
            sem("s_" + n) for n in ("x1st", "x1ve", "x1rms", "x1inv", "xn", "x1save"))
        x1_recip = sem("s_x1recip")
        x1_square, x1_root, x1_norm, x1_scale = (sem("s_x1" + n) for n in ("sq", "root", "norm", "scale"))
        xnT_done, xnT_hi_ready, xnT_lo_ready = sem("s_xnT"), sem("s_xnThi"), sem("s_xnTlo")
        la_done, lb_done, max_ready, neg_hi, neg_ready, maxT_done, rows_ready = (
            sem("s_" + n) for n in ("la", "lb", "max", "neghi", "neg", "maxT", "rows"))
        la_shifted, lb_shifted, disp_ready, comb_ready = (sem("s_" + n) for n in ("las", "lbs", "disp", "comb"))
        slots_done, slots_inv, slots_ready, slT_done, slT_hi_ready, slT_lo_ready = (
            sem("s_" + n) for n in ("sl", "slinv", "slots", "slT", "slThi", "slTlo"))
        hid_done = [sem(f"s_hid{f}") for f in range(FJ)]
        gelu_ready = [sem(f"s_gelu{f}") for f in range(FJ)]
        mix_done = [sem(f"s_mixdone{c}") for c in range(NC)]
        proc_done, proc_ready, mix_inv, mix_ready, mix_stats, mix_var, mix_rstd, mixh_ready, res_ready = (
            sem("s_" + n) for n in ("proc", "procs", "mixinv", "mixs", "mixst", "mixve", "mixrs", "mixh", "res"))
        x_shift, mix_shift, x_neg, mix_neg = (
            sem("s_" + n) for n in ("xshift", "mixshift", "xneg", "mixneg"))
        stored = [sem(f"stored{u}") for u in range(2)]

        def after(eng, s, n):
            if not isinstance(n, int) or 0 <= n < NB:
                eng.wait_ge(s, n + 1)

        def after_apart(eng, s, n):
            value = n + 1 if isinstance(n, int) else eng.to_reg(n + 1)
            eng.wait_ge(s_const, 8)
            eng.wait_ge(s, value)

        def loaded(eng, s, n, u):
            eng.wait_ge(s[u], 16 * (n // 2 + 1) if isinstance(n, int) else 8 * (n - u + 2))

        STAGES = 5
        LOOP_FROM, LOOP_TO = 4, NB - STAGES - 1

        def pipeline(eng, step):
            def short(s):
                step(*[(s + k, (s + k) % 2) if 0 <= s + k < NB else None for k in range(STAGES)])

            for s in range(1 - STAGES, LOOP_FROM):
                short(s)
            with eng.Fori(LOOP_FROM // 2, LOOP_TO // 2) as m:
                for j in range(2):
                    step(*[(2 * m + (j + k), (j + k) % 2) for k in range(STAGES)])
            for s in range(LOOP_TO, NB):
                short(s)

        block = ctx.enter_context(nc.Block())

        @block.sync
        def _(sp):
            for i, w in enumerate((wq, wk, wv, wo)):
                sp.dma_start(w_in[:, i, :], w).then_inc(s_wload, 16)
            for i, b in enumerate((bq, bk, bv, bo)):
                sp.dma_start(b_row[0:1, i * DIM:(i + 1) * DIM], b.rearrange("(a n) -> a n", a=1)).then_inc(s_wload, 16)
            for u in range(2):
                sp.dma_start(X[u][:, :, :], x_v[u]).then_inc(x_loaded[u], 16)
            sp.dma_start(gx_col[:, :], gamma_x.rearrange("(p a) -> p a", a=1)).then_inc(s_seload, 16)
            sp.dma_start(gs_col[:, :], gamma_slot.rearrange("(p a) -> p a", a=1)).then_inc(s_seload, 16)
            se_v = slot_embeds.rearrange("e t d -> (e t) d").rearrange("(j p) d -> p j d", p=P)
            sp.dma_start(se_in[:, :, :], se_v).then_inc(s_seload, 16)
            sp.dma_start(w1_in[:, :], w1).then_inc(s_seload, 16)
            sp.dma_start(w2_in[:, :, :], w2.rearrange("(j p) d -> p j d", p=P)).then_inc(s_seload, 16)

            def row_of(view, n):
                if isinstance(n, int):
                    return view[n]
                return view[bass.ds(n, 1)].rearrange("b p c d -> p (b c) d")

            def store(n, u):
                after(sp, res_ready, n)
                sp.dma_start(row_of(out_v, n), res[u][:, :, :]).then_inc(stored[u], 16)

            def step(b, l, r, t, p):
                if p and not (isinstance(p[0], int) and p[0] + 2 >= NB):
                    n, u = p
                    after(sp, xh_ready, n)
                    sp.dma_start(X[u][:, :, :], row_of(x_v, n + 2)).then_inc(x_loaded[u], 16)
                if t:
                    n, u = t
                    after(sp, x1_ready, n - 2)
                    sp.dma_start(x_res[u][:, :, :], row_of(x_v, n)).then_inc(x_res_loaded[u], 16)
                if b and not (isinstance(b[0], int) and b[0] == 0):
                    store(b[0] - 1, 1 - b[1])

            pipeline(sp, step)
            store(NB - 1, (NB - 1) % 2)
            sp.wait_ge(stored[0], 16 * (NB // 2))
            sp.wait_ge(stored[1], 16 * (NB // 2))

        @block.gpsimd
        def _(pool):
            pool.memset(ident[:, :], 0.0).then_inc(s_const, 1)
            pool.memset(tri_f[:, :], 1.0).then_inc(s_const, 1)
            pool.memset(blockmask[:, :], 0.0).then_inc(s_const, 1)
            pool.memset(ones_r[:, :].bitcast(F32), 1.0)
            pool.memset(ones_f[:, :], 1.0)
            pool.memset(minus_half[:, :], -0.5)
            pool.memset(plus_half[:, :], 0.5)
            for u in range(2):
                pool.memset(xn[u][:, :, DIM:XW], 1.0)
            pool.memset(proc[:, :, DIM:XW], 1.0).then_inc(s_const, 1)
            pool.wait_ge(s_const, 4)
            pool.affine_select(out=ident[:, :], in_=ident[:, :], compare_op=ALU.not_equal, fill=1.0, base=0,
                               pattern=[[-1, P]], channel_multiplier=1).then_inc(s_const, 1)
            pool.affine_select(out=tri_f[:, :], in_=tri_f[:, :], compare_op=ALU.is_ge, fill=0.0, base=0,
                               pattern=[[1, P]], channel_multiplier=-1).then_inc(s_const, 1)
            pool.affine_select(out=blockmask[:, :], in_=blockmask[:, :], compare_op=ALU.not_equal, fill=1.0, base=0,
                               pattern=[[-1, NM]], channel_multiplier=1).then_inc(s_const, 1)
            pool.wait_ge(s_const, 7)
            pool.affine_select(out=blockmask[:, :], in_=blockmask[:, :], compare_op=ALU.not_equal, fill=1.0, base=-NM,
                               pattern=[[-1, NM]], channel_multiplier=1).then_inc(s_const, 1)
            pool.wait_ge(s_sesum, 1)
            pool.tensor_tensor(se_norm[:, :], se_norm[:, :], plus_half[:, :], ALU.pow).then_inc(s_senorm, 1)
            pool.wait_ge(s_senorm, 1)
            pool.tensor_scalar(se_norm[:, :], se_norm[:, :], EPS_RMS, 1.0, ALU.max, ALU.mult).then_inc(s_senorm, 1)

            def rstd(stats_done, var_done, rstd_done, st, n):
                _, mv, ve, rs = st
                after_apart(pool, stats_done, n)
                pool.tensor_scalar(ve[:, :], mv[:, :, 1], EPS_LN, 1.0, ALU.add, ALU.mult).then_inc(var_done, 1)
                after(pool, var_done, n)
                pool.tensor_tensor(rs[:, :], ve[:, :], minus_half[:, 0:NC], ALU.pow).then_inc(rstd_done, 1)

            def shift(st, dst, rstd_done, neg_done, shift_done, n):
                pool.tensor_scalar(neg_mean[:, :], st[1][:, :, 0], -1.0, 0.0, ALU.mult, ALU.add).then_inc(neg_done, 1)
                after(pool, neg_done, n)
                after(pool, rstd_done, n)
                pool.tensor_tensor(dst[:, :], neg_mean[:, :], st[3][:, :], ALU.mult).then_inc(shift_done, 1)

            def x_rstd_shift(n):
                after_apart(pool, xh_ready, n - 1)
                rstd(x_stats, x_var, x_rstd, st_x, n)
                shift(st_x, shift_x, x_rstd, x_neg, x_shift, n)

            def finish(n, u):
                after(pool, mixh_ready, n)
                after(pool, x1_saved, n)
                if not isinstance(n, int) or n >= 2:
                    loaded(pool, stored, n - 2, u)
                pool.tensor_tensor(res[u][:, :, :], mixh[:, :, :], x1_res[u][:, :, :], ALU.add).then_inc(res_ready, 1)

            def step(b, l, r, t, p):
                if t:
                    n, u = t
                    after(pool, kv_built, n)
                    after(pool, k_ready, n)
                    after(pool, cum_done[UN - 1], n - 1)
                    for c in range(NC):
                        after(pool, kv_hi_ready[c], n)
                        pool.tensor_tensor(kv_lo[:, c, :], kv[:, c, :], kv_hi[:, c, :].bitcast(F32), ALU.subtract)\
                            .then_inc(kv_lo_ready[c], 1)
                if b and not (isinstance(b[0], int) and b[0] == 0):
                    finish(b[0] - 1, 1 - b[1])
                if l:
                    n, u = l
                    after_apart(pool, x1_ready, n)
                    after(pool, res_ready, n - 2)
                    pool.tensor_copy(x1_res[u][:, :, :], x1[u][:, :, :]).then_inc(x1_saved, 1)
                if r:
                    rstd(y_stats, y_var, y_rstd, st_y, r[0])
                if p:
                    n, u = p
                    after(pool, k_ready, n)
                    after(pool, biased[NC - 1], n)
                    after(pool, kv_hi_ready[NC - 1], n - 1)
                    after(pool, kv_lo_ready[NC - 1], n - 1)
                    for c in range(NC):
                        k_b = kv[:, c, KVF:FEAT].rearrange("p (h o e) -> p h o e", h=NH, o=1)\
                            .broadcast_to((P, NH, HD, HD))
                        v_b = qkv[:, c, 2 * DIM:QKV].rearrange("p (h d o) -> p h d o", h=NH, o=1)\
                            .broadcast_to((P, NH, HD, HD))
                        last = pool.tensor_tensor(kv[:, c, 0:KVF].rearrange("p (h d e) -> p h d e", h=NH, d=HD),
                                                  k_b, v_b, ALU.mult)
                    last.then_inc(kv_built, 1)
                if r:
                    n, u = r
                    rstd(x1_stats, x1_var, x1_rms, st_1, n)
                    mv, rs = st_1[1], st_1[3]
                    pool.tensor_scalar(root_v[:, :], mv[:, :, 1], float(DIM), 0.0, ALU.mult, ALU.add)\
                        .then_inc(x1_square, 1)
                    after(pool, x1_square, n)
                    pool.tensor_tensor(root_v[:, :], root_v[:, :], plus_half[:, 0:NC], ALU.pow).then_inc(x1_root, 1)
                    after(pool, x1_rms, n)
                    after(pool, x1_root, n)
                    after(pool, x1_inv, n - 1)
                    pool.tensor_tensor(rms_n[:, :], root_v[:, :], rs[:, :], ALU.mult).then_inc(x1_norm, 1)
                if p and not (isinstance(p[0], int) and p[0] + 1 >= NB):
                    x_rstd_shift(p[0] + 1)
                if b:
                    rstd(mix_stats, mix_var, mix_rstd, st_o, b[0])
                    shift(st_o, shift_o, mix_rstd, mix_neg, mix_shift, b[0])

            rstd(x_stats, x_var, x_rstd, st_x, 0)
            shift(st_x, shift_x, x_rstd, x_neg, x_shift, 0)
            pipeline(pool, step)
            finish(NB - 1, (NB - 1) % 2)

        @block.scalar
        def _(act):
            def copy(dst, src):
                return act.activation(dst, src, ACT.Copy)

            def normalise(dst, src, st, shift, done):
                for c in range(NC):
                    last = act.activation(dst[:, c, :], src[:, c, :], ACT.Identity, bias=shift[:, c:c + 1],
                                          scale=st[3][:, c:c + 1])
                last.then_inc(done, 1)

            def mix_norm(n):
                after(act, mix_shift, n)
                after(act, res_ready, n - 1)
                normalise(mixh, mix, st_o, shift_o, mixh_ready)

            def step(b, l, r, t, p):
                if p:
                    n, u = p
                    after(act, x_shift, n)
                    after(act, xT_done, n - 1)
                    normalise(xh, X[u], st_x, shift_x, xh_ready)
                if b:
                    n, u = b
                    for f in range(FJ):
                        after(act, hid_done[f], n)
                        if f == 0:
                            after(act, proc_done, n - 1)
                        act.activation(hid[:, f, :], HB[:, f % 2, :], ACT.Gelu).then_inc(gelu_ready[f], 1)
                if p:
                    n, u = p
                    after(act, xT_done, n)
                    after(act, qkv_done[NC - 1], n - 1)
                    copy(xT_hi[:, :], WB[:, 1, 0:SEQ]).then_inc(xT_hi_ready, 1)
                if b and not (isinstance(b[0], int) and b[0] == 0):
                    mix_norm(b[0] - 1)
                if r:
                    n, u = r
                    after(act, att_T, n)
                    after(act, wo_done, n - 1)
                    copy(attT[:, :], WB[:, 0, 0:SEQ]).then_inc(attT_ready, 1)
                if p:
                    n, u = p
                    after(act, biased[NC - 1], n)
                    after(act, biased[0], n)
                    after(act, kv_hi_ready[NC - 1], n - 1)
                    after(act, kv_lo_ready[NC - 1], n - 1)
                    act.activation(kv[:, :, KVF:FEAT], qkv[:, :, DIM:2 * DIM], ACT.Exp).then_inc(k_ready, 1)
                    after(act, prod_ready[UN - 1], n - 2)
                    act.activation(Q[u][:, :, :], qkv[:, :, 0:DIM], ACT.Exp).then_inc(q_ready, 1)
                if b:
                    n, u = b
                    after(act, proc_done, n)
                    after(act, mix_done[NC - 1], n - 1)
                    copy(proc[:, :, 0:DIM], PR).then_inc(proc_ready, 1)
                if l:
                    n, u = l
                    after(act, la_shifted, n)
                    after(act, slots_done, n - 1)
                    for c in range(NC):
                        last = act.activation(disp[:, c, :], LA[:, c, :], ACT.Exp)
                    last.then_inc(disp_ready, 1)
                    after(act, lb_shifted, n)
                    after(act, mix_done[NC - 1], n - 2)
                    for g in range(2):
                        last = act.activation(comb[u][:, 2 * g:2 * g + 2, :], LBv[:, 2 * g:2 * g + 2, :], ACT.Exp)
                    last.then_inc(comb_ready, 1)
                act.preload_act_table(ACT.Gelu)
                if p:
                    n, u = p
                    after(act, kv_built, n)
                    after(act, k_ready, n)
                    after(act, cum_done[UN - 1], n - 1)
                    copy(kv_hi[:, 0, :], kv[:, 0, :]).then_inc(kv_hi_ready[0], 1)
                if l:
                    n, u = l
                    after(act, slT_done, n)
                    after(act, hid_done[FJ - 1], n - 1)
                    copy(slT_hi[:, :], LB[:, 0, :]).then_inc(slT_hi_ready, 1)
                if p:
                    copy(kv_hi[:, 1, :], kv[:, 1, :]).then_inc(kv_hi_ready[1], 1)
                if r:
                    n, u = r
                    after(act, xnT_done, n)
                    after(act, lb_done, n - 1)
                    copy(xnT_hi[:, :], WB[:, 0, 0:SEQ]).then_inc(xnT_hi_ready, 1)

            pipeline(act, step)
            mix_norm(NB - 1)

        @block.tensor
        def _(pe):
            pe.wait_ge(s_const, 8)
            pe.wait_ge(s_wload, 16 * 8)
            for i in range(4):
                last = pe.transpose(WB[:, 0, i * P:(i + 1) * P], w_in[:, i, :], ident[:, :])
            last.then_inc(s_pe0, 1)
            pe.matmul(WB[:, 1, :], ones_f[0:1, :], b_row[0:1, :], start=True, stop=True).then_inc(s_pe0, 1)
            pe.wait_ge(s_dve0, 1)
            for j in range(SJ):
                last = pe.transpose(LA[:, 0, j * P:(j + 1) * P], se_in[:, j, :], ident[:, :])
            last.then_inc(s_pe0, 1)
            pe.wait_ge(s_setup, 1)

            def three(dst, a_hi, a_lo, b_hi, b_lo, start=True, stop=True):
                pe.matmul(dst, a_hi, b_hi, start=start, stop=False, skip_group_check=True)
                pe.matmul(dst, a_hi, b_lo, start=False, stop=False, skip_group_check=True)
                return pe.matmul(dst, a_lo, b_hi, start=False, stop=stop, skip_group_check=True)

            def hidden(n, u):
                after(pe, slT_hi_ready, n)
                after(pe, slT_lo_ready, n)
                for f in range(FJ):
                    if f == 0:
                        after(pe, proc_ready, n - 1)
                    elif f == 1:
                        after(pe, mix_ready, n - 1)
                    else:
                        after(pe, gelu_ready[f - 2], n)
                    cols = slice(f * P, (f + 1) * P)
                    three(HB[:, f % 2, :], w1_hi[:, cols], w1_lo[:, cols], slT_hi[:, :], slT_lo[:, :])\
                        .then_inc(hid_done[f], 1)

            def x_transpose(n, u):
                after(pe, xh_ready, n)
                after(pe, prod_ready[4], n - 2)
                if isinstance(n, int):
                    after(pe, biased[0], n - 1)
                for c in range(NC):
                    last = pe.transpose(WB[:, 1, c * P:(c + 1) * P], xh[:, c, :], ident[:, :])
                last.then_inc(xT_done, 1)

            def att_transpose(n, u):
                after(pe, att_ready, n)
                after(pe, xnT_hi_ready, n - 1)
                after(pe, xnT_lo_ready, n - 1)
                if isinstance(n, int):
                    after(pe, biased[1], n + 1)
                for c in range(NC):
                    last = pe.transpose(WB[:, 0, c * P:(c + 1) * P], att[:, c, :], ident[:, :])
                last.then_inc(att_T, 1)

            def project(n, u):
                after(pe, xT_hi_ready, n)
                after(pe, xT_lo_ready, n)
                for c in range(NC):
                    if c == 1:
                        after(pe, attT_ready, n - 2)
                        if isinstance(n, int):
                            after(pe, biased[1], n - 1)
                            after(pe, prod_ready[3], n - 2)
                    cols = slice(c * P, (c + 1) * P)
                    three(WB[:, 1 - c, 0:QKV], xT_hi[:, cols], xT_lo[:, cols], wqkv_hi[:, :], wqkv_lo[:, :])\
                        .then_inc(qkv_done[c], 1)

            def max_transpose(n, u):
                after(pe, neg_ready, n)
                after(pe, biased[0], n + 3)
                if isinstance(n, int):
                    after(pe, prod_ready[4], n + 1)
                pe.transpose(WB[0:2 * NM, 1, 0:P], neg_max[:, :].bitcast(F32), ident[:, :]).then_inc(maxT_done, 1)

            def attention_out(n, u):
                after(pe, attT_ready, n)
                after(pe, biased[1], n + 2)
                for c in range(NC):
                    last = pe.matmul(WB[:, 0, c * DIM:(c + 1) * DIM], attT[:, c * P:(c + 1) * P], wo_t[:, :],
                                     start=True, stop=True)
                last.then_inc(wo_done, 1)

            def cumulate(n, u, k):
                if k == 0:
                    after(pe, kv_hi_ready[0], n)
                    after(pe, kv_lo_ready[0], n)
                    after(pe, rows_ready, n - 2)
                    if isinstance(n, int):
                        after(pe, biased[0], n + 1)
                elif k == 1:
                    after(pe, y_ready, n - 1)
                    if isinstance(n, int):
                        after(pe, biased[1], n + 1)
                else:
                    after(pe, prod_ready[k - 2], n)
                    if k == 2:
                        after(pe, kv_hi_ready[1], n)
                        after(pe, kv_lo_ready[1], n)
                bank = (k + 1) % 2
                if k < 2 * NC:
                    c, f = k // 2, slice((k % 2) * HALF, (k % 2 + 1) * HALF)
                    tiles = [(c, WB[:, bank, 0:HALF], f)]
                else:
                    tiles = [(c, WB[:, bank, c * DIM:(c + 1) * DIM], slice(KVF, FEAT)) for c in range(NC)]
                for c, dst, f in tiles:
                    terms = [(ones_r, a[:, e, f]) for e in range(c) for a in (kv_hi, kv_lo)]
                    terms += [(tri, a[:, c, f]) for a in (kv_hi, kv_lo)]
                    for i, (m, a) in enumerate(terms):
                        last = pe.matmul(dst, m[:, :], a, start=(i == 0), stop=(i == len(terms) - 1))
                last.then_inc(cum_done[k], 1)

            def xn_transpose(n, u):
                after(pe, xn_ready, n)
                after(pe, prod_ready[3], n + 1)
                for c in range(NC):
                    last = pe.transpose(WB[:, 0, c * P:(c + 1) * P], xn[u][:, c, 0:DIM], ident[:, :])
                last.then_inc(xnT_done, 1)

            def logits(n, u):
                after(pe, xnT_hi_ready, n)
                after(pe, xnT_lo_ready, n)
                after(pe, slots_ready, n - 1)
                after(pe, slT_hi_ready, n - 1)
                after(pe, slT_lo_ready, n - 1)
                for c in range(NC):
                    cols = slice(c * P, (c + 1) * P)
                    last = three(LA[:, c, :], xnT_hi[:, cols], xnT_lo[:, cols], se_hi[:, :], se_lo[:, :], stop=False)
                last.then_inc(la_done, 1)
                for j in range(SJ):
                    cols = slice(j * P, (j + 1) * P)
                    last = three(LBv[:, j, :], se_hi[:, cols], se_lo[:, cols], xnT_hi[:, :], xnT_lo[:, :],
                                 start=(j % 2 == 0), stop=False)
                last.then_inc(lb_done, 1)

            def subtract_max(n, u):
                after(pe, rows_ready, n)
                rows_f = max_rows[:, :, :].rearrange("p m t -> p (m t)")
                for c in range(NC):
                    last = pe.matmul(LA[:, c, :], ones_r[0:2 * NM, :], rows_f[:, 0:SLOTS], start=False, stop=True,
                                     skip_group_check=True)
                last.then_inc(la_shifted, 1)
                for j in range(SJ):
                    last = pe.matmul(LBv[:, j, :], ones_r[0:2 * NM, :], rows_f[:, SLOTS:SLOTS + SEQ], start=False,
                                     stop=True, skip_group_check=True)
                last.then_inc(lb_shifted, 1)

            def gather_slots(n, u):
                after(pe, disp_ready, n)
                for j in range(SJ):
                    for c in range(NC):
                        last = pe.matmul(SL[:, j // 2, j % 2, 0:DIM + 1], disp[:, c, j * P:(j + 1) * P],
                                         xn[u][:, c, 0:DIM + 1], start=(c == 0), stop=(c == NC - 1))
                last.then_inc(slots_done, 1)

            def slots_transpose(n, u):
                after(pe, slots_ready, n)
                after(pe, comb_ready, n)
                for j in range(SJ):
                    last = pe.transpose(LB[:, 0, j * P:(j + 1) * P], slots[:, j, :], ident[:, :])
                last.then_inc(slT_done, 1)

            def process(n, u, tiles):
                for f in range(FJ):
                    after(pe, gelu_ready[f], n)
                for j in tiles:
                    for f in range(FJ):
                        last = pe.matmul(PR[:, j, :], hid[:, f, j * P:(j + 1) * P], w2_in[:, f, :],
                                         start=(f == 0), stop=(f == FJ - 1))
                if tiles[-1] == SJ - 1:
                    last.then_inc(proc_done, 1)

            def mixture(n, u, c):
                after(pe, proc_ready, n)
                after(pe, comb_ready, n)
                for j in range(SJ):
                    last = pe.matmul(OB[:, c, 0:DIM + 1], comb[u][:, j, c * P:(c + 1) * P],
                                     proc[:, j, 0:DIM + 1], start=(j == 0), stop=(j == SJ - 1))
                last.then_inc(mix_done[c], 1)

            def step(b, l, r, t, p):
                if b:
                    hidden(*b)
                if p:
                    x_transpose(*p)
                if l:
                    logits(*l)
                if r:
                    att_transpose(*r)
                if p:
                    project(*p)
                if b:
                    process(*b, (0, 1))
                if l:
                    max_transpose(*l)
                if r:
                    attention_out(*r)
                if b:
                    process(*b, (2, 3))
                if t:
                    cumulate(*t, 0)
                if l:
                    subtract_max(*l)
                if t:
                    for k in range(1, 4):
                        cumulate(*t, k)
                if l:
                    gather_slots(*l)
                if t:
                    for k in range(4, UN):
                        cumulate(*t, k)
                if l:
                    slots_transpose(*l)
                if b:
                    mixture(*b, 0)
                if r:
                    xn_transpose(*r)
                if b:
                    mixture(*b, 1)

            pipeline(pe, step)

        @block.vector
        def _(dve):
            dve.wait_ge(s_const, 8)
            dve.tensor_copy(tri[:, :], tri_f[:, :])
            dve.wait_ge(s_seload, 16 * 5)
            dve.tensor_tensor(se_sq[:, :, :], se_in[:, :, :], se_in[:, :, :], ALU.mult).then_inc(s_dve0s, 1)
            dve.wait_ge(s_dve0s, 1)
            dve.tensor_reduce(se_norm[:, :], se_sq[:, :, :], AX.X, ALU.add).then_inc(s_sesum, 1)
            dve.tensor_scalar(w1_in[:, :], w1_in[:, :], gx_col[:, 0:1], None, ALU.mult).then_inc(s_dve0s, 1)
            dve.wait_ge(s_dve0s, 2)
            dve.tensor_copy(w1_hi[:, :], w1_in[:, :]).then_inc(s_dve0s, 1)
            dve.wait_ge(s_dve0s, 3)
            dve.tensor_tensor(w1_lo[:, :], w1_in[:, :], w1_hi[:, :].bitcast(F32), ALU.subtract)
            dve.wait_ge(s_senorm, 2)
            dve.reciprocal(se_norm[:, :], se_norm[:, :]).then_inc(s_dve0s, 1)
            dve.wait_ge(s_dve0s, 4)
            dve.tensor_scalar(se_norm[:, :], se_norm[:, :], ROOT_DIM, None, ALU.mult).then_inc(s_dve0s, 1)
            dve.wait_ge(s_dve0s, 5)
            dve.tensor_tensor(se_in[:, :, :], se_in[:, :, :],
                              se_norm[:, :].rearrange("p (j o) -> p j o", o=1).broadcast_to((P, SJ, DIM)),
                              ALU.mult).then_inc(s_dve0, 1)
            dve.wait_ge(s_pe0, 1)
            dve.tensor_copy(wqkv_hi[:, :], WB[:, 0, 0:QKV]).then_inc(s_dve0s, 1)
            dve.tensor_copy(wo_t[:, :], WB[:, 0, QKV:QKV + DIM])
            dve.wait_ge(s_dve0s, 6)
            dve.tensor_tensor(wqkv_lo[:, :], WB[:, 0, 0:QKV], wqkv_hi[:, :].bitcast(F32), ALU.subtract)
            dve.wait_ge(s_pe0, 2)
            dve.tensor_copy(bias[:, :], WB[:, 1, :]).then_inc(s_dve0s, 1)
            dve.wait_ge(s_pe0, 3)
            dve.tensor_scalar(se_f[:, :], LA[:, 0, :], gx_col[:, 0:1], gs_col[:, 0:1], ALU.mult, ALU.mult)\
                .then_inc(s_dve0s, 1)
            dve.wait_ge(s_dve0s, 8)
            dve.tensor_copy(se_hi[:, :], se_f[:, :]).then_inc(s_dve0s, 1)
            dve.wait_ge(s_dve0s, 9)
            dve.tensor_tensor(se_lo[:, :], se_f[:, :], se_hi[:, :].bitcast(F32), ALU.subtract).then_inc(s_setup, 1)

            def low_part(dst, a, hi):
                return dve.tensor_tensor(dst, a, hi.bitcast(F32), ALU.subtract)

            def stats(st, src, ready, done, n, chain):
                s6, mv = st[0], st[1]
                if ready is not None:
                    after(dve, ready, n)
                for c in range(NC):
                    last = dve.bn_stats(s6[:, c, :], src[:, c, :])
                last.then_inc(chain, 1)
                after_apart(dve, chain, n)
                for c in range(NC):
                    last = dve.bn_aggr(mv[:, c, :], s6[:, c, :])
                last.then_inc(done, 1)

            x_chain, y_chain, x1_chain, mix_chain = (sem("s_ch" + n) for n in ("x", "y", "x1", "mix"))

            def normalise(dst, src, st, done):
                mv, rs = st[1], st[3]
                for c in range(NC):
                    last = dve.tensor_scalar(dst[:, c, :], src[:, c, :], mv[:, c, 0:1], rs[:, c:c + 1],
                                             ALU.subtract, ALU.mult)
                last.then_inc(done, 1)

            def x_stat(n, u):
                loaded(dve, x_loaded, n, u)
                after(dve, x_shift, n - 1)
                stats(st_x, X[u], None, x_stats, n, x_chain)

            def multiply(n, u, k):
                after(dve, cum_done[k], n)
                bank = (k + 1) % 2
                if k < 2 * NC:
                    c, g = k // 2, k % 2
                    q_b = Q[u][:, c, g * HH * HD:(g + 1) * HH * HD].rearrange("p (h o e) -> p h o e", h=HH, o=1)\
                        .broadcast_to((P, HH, HD, HD))
                    dve.tensor_tensor(prod[:, c, g * HALF:(g + 1) * HALF].rearrange("p (h d e) -> p h d e", h=HH, d=HD),
                                      WB[:, bank, 0:HALF].rearrange("p (h d e) -> p h d e", h=HH, d=HD),
                                      q_b, ALU.mult).then_inc(prod_ready[k], 1)
                else:
                    dve.tensor_tensor(prod[:, :, KVF:FEAT], WB[:, bank, 0:NC * DIM].rearrange("p (c d) -> p c d", c=NC),
                                      Q[u][:, :, :], ALU.mult).then_inc(prod_ready[k], 1)

            def attention(n, u):
                for k in range(UN):
                    after(dve, prod_ready[k], n)
                dve.tensor_reduce(numden[:, :, :], prod[:, :, :].rearrange("p c (f e) -> p c f e", e=HD),
                                  AX.X, ALU.add).then_inc(summed, 1)
                after(dve, summed, n)
                dve.reciprocal(den_inv[:, :, :], numden[:, :, DIM:DIM + NH]).then_inc(den_ready, 1)
                after(dve, den_ready, n)
                after(dve, att_T, n - 1)
                dve.tensor_tensor(att[:, :, :].rearrange("p c (h d) -> p c h d", h=NH),
                                  numden[:, :, 0:DIM].rearrange("p c (h d) -> p c h d", h=NH),
                                  den_inv[:, :, :].rearrange("p c (h o) -> p c h o", o=1)
                                  .broadcast_to((P, NC, NH, HD)), ALU.mult).then_inc(att_ready, 1)

            def maxima_rows(n, u):
                after(dve, maxT_done, n)
                after(dve, lb_shifted, n - 1)
                dve.tensor_tensor(max_rows[:, :, :],
                                  WB[0:2 * NM, 1, 0:P].rearrange("p (o t) -> p o t", o=1).broadcast_to((2 * NM, NM, P)),
                                  blockmask[:, :].rearrange("p (m o) -> p m o", o=1).broadcast_to((2 * NM, NM, P)),
                                  ALU.mult).then_inc(rows_ready, 1)

            def row_maxima(n, u):
                after(dve, la_done, n)
                after(dve, neg_ready, n - 1)
                dve.tensor_reduce(maxima[:, SJ:NM], LA[:, :, :], AX.X, ALU.max)
                after(dve, lb_done, n)
                dve.tensor_reduce(maxima[:, 0:SJ], LBv, AX.X, ALU.max).then_inc(max_ready, 1)
                after(dve, max_ready, n)
                after(dve, maxT_done, n - 1)
                dve.tensor_scalar(neg_max[:, 0:NM], maxima[:, :], -1.0, None, ALU.mult).then_inc(neg_hi, 1)
                after(dve, neg_hi, n)
                dve.scalar_tensor_tensor(out=neg_max[:, NM:2 * NM], in0=maxima[:, :], scalar=-1.0,
                                         in1=neg_max[:, 0:NM].bitcast(F32), op0=ALU.mult, op1=ALU.subtract)\
                    .then_inc(neg_ready, 1)

            def step(b, l, r, t, p):
                if r:
                    attention(*r)
                if p:
                    n, u = p
                    after(dve, xT_hi_ready, n)
                    after(dve, qkv_done[NC - 1], n - 1)
                    low_part(xT_lo[:, :], WB[:, 1, 0:SEQ], xT_hi[:, :]).then_inc(xT_lo_ready, 1)
                if l:
                    row_maxima(*l)
                if p:
                    n, u = p
                    after(dve, kv_built, n - 1)
                    after(dve, q_ready, n - 1)
                    for c in range(NC):
                        after(dve, qkv_done[c], n)
                        dve.tensor_tensor(qkv[:, c, :], WB[:, 1 - c, 0:QKV], bias[:, 0:QKV], ALU.add)\
                            .then_inc(biased[c], 1)
                if l:
                    maxima_rows(*l)
                if r:
                    n, u = r
                    after(dve, wo_done, n)
                    dve.tensor_tensor(y[:, :, :], WB[:, 0, 0:NC * DIM].rearrange("p (c d) -> p c d", c=NC),
                                      bias[:, QKV:QKV + DIM].rearrange("p (o d) -> p o d", o=1)
                                      .broadcast_to((P, NC, DIM)), ALU.add).then_inc(y_ready, 1)
                    stats(st_y, y, y_ready, y_stats, n, y_chain)
                if p and not (isinstance(p[0], int) and p[0] + 1 >= NB):
                    x_stat(p[0] + 1, 1 - p[1])
                if t:
                    n, u = t
                    after(dve, q_ready, n)
                    after(dve, summed, n - 1)
                    multiply(n, u, 0)
                    multiply(n, u, 1)
                if r:
                    n, u = r
                    after(dve, y_rstd, n)
                    normalise(y, y, st_y, yh_ready)
                    after(dve, yh_ready, n)
                    loaded(dve, x_res_loaded, n, u)
                    after(dve, x1_saved, n - 2)
                    after(dve, xn_ready, n - 2)
                    dve.tensor_tensor(x1[u][:, :, :], y[:, :, :], x_res[u][:, :, :], ALU.add).then_inc(x1_ready, 1)
                    stats(st_1, x1[u], x1_ready, x1_stats, n, x1_chain)
                if t:
                    n, u = t
                    multiply(n, u, 2)
                    multiply(n, u, 3)
                if l:
                    n, u = l
                    after(dve, slots_done, n)
                    dve.reciprocal(disp_inv[:, :].rearrange("p (g j) -> p g j", g=2), SL[:, :, :, DIM])\
                        .then_inc(slots_inv, 1)
                    after(dve, slots_inv, n)
                    after(dve, slT_done, n - 1)
                    dve.tensor_tensor(slots[:, :, :].rearrange("p (g j) d -> p g j d", g=2), SL[:, :, :, 0:DIM],
                                      disp_inv[:, :].rearrange("p (g j o) -> p g j o", g=2, o=1)
                                      .broadcast_to((P, 2, 2, DIM)), ALU.mult).then_inc(slots_ready, 1)
                if t:
                    n, u = t
                    multiply(n, u, 4)
                if r:
                    n, u = r
                    after(dve, x1_norm, n)
                    dve.tensor_scalar(rms_n2[:, :], rms_n[:, :], EPS_RMS, 1.0 / ROOT_DIM, ALU.max, ALU.mult)\
                        .then_inc(x1_inv, 1)
                    after(dve, x1_inv, n)
                    dve.reciprocal(rms_inv[:, :], rms_n2[:, :]).then_inc(x1_recip, 1)
                    after(dve, x1_recip, n)
                    after(dve, x1_rms, n)
                    dve.tensor_tensor(scale_n[:, :], rms_inv[:, :], st_1[3][:, :], ALU.mult).then_inc(x1_scale, 1)
                    after(dve, x1_scale, n)
                    after(dve, slots_done, n - 2)
                    for c in range(NC):
                        last = dve.tensor_scalar(xn[u][:, c, 0:DIM], x1[u][:, c, :], st_1[1][:, c, 0:1],
                                                 scale_n[:, c:c + 1], ALU.subtract, ALU.mult)
                    last.then_inc(xn_ready, 1)
                if l:
                    n, u = l
                    after(dve, slT_hi_ready, n)
                    after(dve, hid_done[FJ - 1], n - 1)
                    low_part(slT_lo[:, :], LB[:, 0, :], slT_hi[:, :]).then_inc(slT_lo_ready, 1)
                if r:
                    n, u = r
                    after(dve, xnT_hi_ready, n)
                    after(dve, lb_done, n - 1)
                    low_part(xnT_lo[:, :], WB[:, 0, 0:SEQ], xnT_hi[:, :]).then_inc(xnT_lo_ready, 1)
                if b:
                    n, u = b
                    after(dve, mix_done[0], n)
                    after(dve, mix_done[1], n)
                    dve.reciprocal(comb_inv[:, :], OB[:, :, DIM]).then_inc(mix_inv, 1)
                    after(dve, mix_inv, n)
                    after(dve, mixh_ready, n - 1)
                    dve.tensor_tensor(mix[:, :, :], OB[:, :, 0:DIM],
                                      comb_inv[:, :].rearrange("p (c o) -> p c o", o=1).broadcast_to((P, NC, DIM)),
                                      ALU.mult).then_inc(mix_ready, 1)
                    stats(st_o, mix, mix_ready, mix_stats, n, mix_chain)

            x_stat(0, 0)
            pipeline(dve, step)


_INS = ["L0_attn_x", "L0_attn_Wq", "L0_attn_bq", "L0_attn_Wk", "L0_attn_bk", "L0_attn_Wv", "L0_attn_bv",
        "L0_attn_Wo", "L0_attn_bo", "L0_ffn_gamma_x", "L0_ffn_gamma_slot", "L0_ffn_slot_embeds",
        "L0_ffn_w1", "L0_ffn_w2"]


def kernel(**inputs):
    import numpy as _np
    import concourse.bacc as _bacc
    from concourse import mybir as _mybir
    from concourse.bass_utils import run_bass_kernel_spmd as _run

    nc = _bacc.Bacc("TRN2", target_bir_lowering=False, num_devices=1)
    arrays, args = {}, []
    for name in _INS:
        a = _np.ascontiguousarray(inputs[name])
        arrays[f"in_{name}_dram"] = a
        args.append(nc.dram_tensor(f"in_{name}_dram", a.shape, _mybir.dt.from_np(a.dtype), kind="ExternalInput").ap())
    shape = inputs["L0_attn_x"].shape
    args.append(nc.dram_tensor("out_0_dram", shape, _mybir.dt.float32, kind="ExternalOutput").ap())
    attention_and_slot_mixture(nc, *args)
    r = _run(nc, [arrays], core_ids=[0])
    return r.results[0]["out_0_dram"]
```
